# Optimizing a Trainium2 kernel written in Bass

```python
import numpy as np
import jax
import jax.numpy as jnp

def _softmax(x, axis=-1):
    return jax.nn.softmax(x, axis=axis)

def _gelu(x):
    return jax.nn.gelu(x, approximate=True)

def _silu(x):
    return jax.nn.silu(x)

def _sigmoid(x):
    return jax.nn.sigmoid(x)

def _layernorm(x, axis=-1, eps=1e-05):
    m = jnp.mean(x, axis=axis, keepdims=True)
    v = jnp.var(x, axis=axis, keepdims=True)
    return (x - m) / jnp.sqrt(v + eps)

def _scatter_add(tgt, idx, src, axis=0):
    return tgt.at[idx].add(src)

def _segment_sum(src, seg, n):
    return jax.ops.segment_sum(src, seg, n)
kernel_name = 'mk_gnn_resnorm_d1_gnn_r8_db2771'

def setup_inputs(seed: int=0):
    np.random.seed(seed)
    _w = jnp.asarray

    def _rec_inputs():
        import jax
        import jax.numpy as jnp
        _gk = jax.random.key(seed)
        x = -0.000202 + 1 * jax.random.normal(jax.random.fold_in(_gk, 1), (6250, 128), jnp.float32)
        _s = jax.random.randint(jax.random.fold_in(_gk, 2), (100000,), 0, 6250, jnp.int32)
        _d = jax.random.randint(jax.random.fold_in(_gk, 3), (100000,), 0, 6250, jnp.int32)
        _loop = jnp.arange(6250, dtype=jnp.int32)
        src = jnp.concatenate([_s, _d, _loop])
        dst = jnp.concatenate([_d, _s, _loop])
        _o = jnp.argsort(dst, stable=True)
        src = src[_o]
        dst = dst[_o]
        edge_attr_128 = -6.47781e-05 + 0.999943 * jax.random.normal(jax.random.fold_in(_gk, 11), (206250, 128), jnp.float32)
        return (x, src, dst, edge_attr_128)
    x, src, dst, edge_attr_128 = _rec_inputs()

    def _L0_gnn_setup():
        import jax, jax.numpy as jnp
        import numpy as np
        N_NODES = 6250
        N_EDGES = 200000
        DIM_H = 128
        N_HEADS = 8
        OUT_DIM = DIM_H // N_HEADS
        key = jax.random.key(seed)
        ks = jax.random.split(key, 7)
        scale = 1.0 / np.sqrt(DIM_H)
        return {'h': jax.random.normal(ks[0], (N_NODES, DIM_H), dtype=jnp.float32), 'edge_attr': jax.random.normal(ks[1], (N_EDGES, DIM_H), dtype=jnp.float32), 'WQ': jax.random.normal(ks[2], (DIM_H, DIM_H), dtype=jnp.float32) * scale, 'WK': jax.random.normal(ks[3], (DIM_H, DIM_H), dtype=jnp.float32) * scale, 'WV': jax.random.normal(ks[4], (DIM_H, DIM_H), dtype=jnp.float32) * scale, 'WE': jax.random.normal(ks[5], (DIM_H, DIM_H), dtype=jnp.float32) * scale, 'edge_index': jax.random.randint(ks[6], (2, N_EDGES), 0, N_NODES, dtype=jnp.int64)}
    _L0_gnn_all = _L0_gnn_setup()
    _L0_gnn_in = {k: v for k, v in _L0_gnn_all.items() if k in ('WQ', 'WK', 'WV', 'WE')}
    del _L0_gnn_all
    return {'x': x, 'src': src, 'dst': dst, 'edge_attr_128': edge_attr_128, 'L0_gnn_WQ': _L0_gnn_in['WQ'], 'L0_gnn_WK': _L0_gnn_in['WK'], 'L0_gnn_WV': _L0_gnn_in['WV'], 'L0_gnn_WE': _L0_gnn_in['WE']}

def reference(x, src, dst, edge_attr_128, L0_gnn_WQ, L0_gnn_WK, L0_gnn_WV, L0_gnn_WE):
    import jax
    import jax.numpy as jnp

    def _L0_gnn_ref(h, edge_attr, WQ, WK, WV, WE, edge_index):
        import jax, jax.numpy as jnp
        import numpy as np
        N_NODES = 6250
        N_EDGES = 200000
        DIM_H = 128
        N_HEADS = 8
        OUT_DIM = DIM_H // N_HEADS
        N = h.shape[0]
        H, D = (N_HEADS, OUT_DIM)
        Qh = (h @ WQ).reshape(N, H, D)
        Kh = (h @ WK).reshape(N, H, D)
        Vh = (h @ WV).reshape(N, H, D)
        Eh = (edge_attr @ WE).reshape(-1, H, D)
        src, dst = (edge_index[0], edge_index[1])
        inv_sqrt_d = 1.0 / np.sqrt(D).astype(np.float32)
        score = jnp.einsum('ehd,ehd,ehd->eh', Kh[src], Qh[dst], Eh) * inv_sqrt_d
        score = jnp.exp(jnp.clip(score, -5.0, 5.0))
        msg = Vh[src] * score[:, :, None]
        wV = jax.ops.segment_sum(msg, dst, num_segments=N)
        Z = jax.ops.segment_sum(score, dst, num_segments=N)
        h_out = wV / (Z[:, :, None] + 1e-06)
        return h_out.reshape(N, H * D)
    edge_index = jnp.stack([src, dst])
    x = _layernorm(x + _L0_gnn_ref(x, edge_attr_128, L0_gnn_WQ, L0_gnn_WK, L0_gnn_WV, L0_gnn_WE, edge_index), axis=-1)
    return x

_drawn_inputs = setup_inputs


def setup_inputs(seed=0):
    import zlib

    import numpy as np

    out = dict(_drawn_inputs(seed))
    spreads = {}
    factors = {}
    for name, (base, spread) in spreads.items():
        noise = np.random.default_rng([zlib.crc32(name.encode()), seed]).standard_normal(out[name].shape)
        drawn = base * np.exp(spread * noise) if base else spread * noise
        out[name] = jnp.asarray(drawn.astype(out[name].dtype))
    for name, factor in factors.items():
        out[name] = (out[name] * factor).astype(out[name].dtype)
    return out
```

```python
from contextlib import ExitStack

import concourse.bass as bass
from concourse import mybir

P = 128
F32 = mybir.dt.float32
BF16 = mybir.dt.bfloat16
I32 = mybir.dt.int32
U32 = mybir.dt.uint32
ALU = mybir.AluOpType
ACT = mybir.ActivationFunctionType
AX = mybir.AxisListType

HEADS = 8
RINGS = 4
BIG = 1.0e6
NOT_AN_EDGE = 0.5
SCORE_LIMIT = 5.0
Z_EPS = 1e-6
LN_EPS = 1e-5


def past(g, n):
    return g >= n if isinstance(g, int) else True


def graph_attention_layernorm(nc, x, src, dst, edge_attr, wq, wk, wv, we, out):
    n_nodes, dim = x.shape
    n_edges = src.shape[0]
    TILES = 4
    GROUP = TILES * P
    G = -(-n_edges // GROUP)
    REPEATED = G * GROUP - n_edges
    GC = -(-G // P)
    LAST_ROW = (G - 1) % P
    WIN = -(-n_nodes // P)
    ODD = WIN - 1
    SLOTS = WIN + ODD
    LAST_NODES = n_nodes - (WIN - 1) * P
    DH = dim // HEADS
    MW = dim + HEADS
    SCALE = float(DH) ** -0.5
    assert dim == P and SCALE == 0.25
    CW = 4
    CH = -(-WIN // CW)
    HALF = P // 2
    FW = 7
    FC = WIN // FW
    assert FC * FW == WIN
    B_LAST = G // RINGS

    def chunk_windows(c):
        return min(CW, WIN - c * CW)

    q_odd_dmas = sum((c * CW < ODD) + 1 for c in range(CH))

    def edge0(g):
        return min(g * GROUP, n_edges - GROUP) if isinstance(g, int) else g * GROUP

    kv_table = nc.dram_tensor("kv_table", [n_nodes, 2 * dim], F32).ap()

    with ExitStack() as ctx:
        def sb(name, shape, dt=F32):
            return ctx.enter_context(nc.sbuf_tensor(name, shape, dt))

        def pb(name, shape):
            return ctx.enter_context(nc.psum_tensor(name, shape, F32))

        def sem(name):
            return ctx.enter_context(nc.semaphore(name))

        xT = sb("xT", [P, WIN * P])
        acc = sb("acc", [P, SLOTS, MW])
        Qp = sb("Qp", [P, SLOTS, 3, dim], BF16)
        kv = sb("kv", [P, RINGS, TILES, 2 * dim])
        src_idx = sb("src_idx", [P, RINGS, TILES], U32)
        attr = sb("attr", [P, 2, TILES, dim])
        attrT = sb("attrT", [P, 2, GROUP])
        hot = sb("hot", [P, RINGS, TILES, P])
        hotT = sb("hotT", [P, 2, GROUP], BF16)
        prod = sb("prod", [P, GROUP])
        msg = sb("msg", [P, 2, TILES, MW])
        score = sb("score", [P, TILES * HEADS])
        clipped = sb("clipped", [P, TILES * HEADS])
        local = sb("local", [P, TILES, G])
        home = sb("home", [P, GC * P])
        table = sb("table", [1, 3, G + 1], I32)
        iota = sb("iota", [P, P])
        ident = sb("ident", [P, P])
        w_kv = sb("w_kv", [P, 2 * dim])
        w_q = sb("w_q", [P, dim])
        w_e = sb("w_e", [P, dim])
        hcol = sb("hcol", [P, GC], I32)
        odd_col = sb("odd_col", [P, GC], I32)
        pair_col = sb("pair_col", [P, GC], I32)
        home_col = sb("home_col", [P, GC])
        slot_col = sb("slot_col", [P, GC])
        least = sb("least", [P, GC])
        most = sb("most", [P, GC])
        stray_col = sb("stray_col", [P, GC])
        cur = sb("cur", [P, 2, TILES])
        zinv = sb("zinv", [P, FW, HEADS])
        stats = sb("stats", [P, FW, 6])
        mean_var = sb("mean_var", [P, 2, FW, 2])
        std = sb("std", [P, 2, FW])
        rstd = sb("rstd", [P, 2, FW])
        shift = sb("shift", [P, 2, FW])
        ln_eps = sb("ln_eps", [P, 1])
        x_in = hot[:, :, :, :]
        x_last = prod[:, 0:dim]
        q_rest = attrT[:, :, :]
        stray_row = msg[0:1, 0, :, :].rearrange("p t m -> p (t m)")[:, 0:G]
        stray_sum = msg[0:1, 1, :, :].rearrange("p t m -> p (t m)")[:, 0:G]
        rows = Qp[:, :, :, :].rearrange("p s t d -> p (s t d)").bitcast(F32)[:, SLOTS * 3 * dim // 2 - GC * GROUP:]
        dst_rows = rows.bitcast(I32).rearrange("p (c e) -> p c e", c=GC)
        local_rows = rows.rearrange("p (c e) -> p c e", c=GC)
        moved = Qp[:, :, :, :].rearrange("p s t d -> p (s t d)").bitcast(F32)[:, 0:WIN * MW]\
            .rearrange("p (w m) -> p w m", m=MW)
        normed = Qp[:, :, :, :].rearrange("p s t d -> p (s t d)").bitcast(F32)[:, WIN * MW:WIN * MW + WIN * dim]\
            .rearrange("p (w m) -> p w m", m=dim)

        psT = pb("psT", [P, GROUP])
        psH = pb("psH", [P, GROUP])
        psE = pb("psE", [P, 2, GROUP])
        psQ = pb("psQ", [P, 2, GROUP])
        psW = pb("psW", [P, 2, GROUP])
        psX = [psT, psH]

        rows_zero = sem("rows_zero")
        x_zero = sem("x_zero")
        const_ready = sem("const_ready")
        id_zero = sem("id_zero")
        first_ok = sem("first_ok")
        acc_zero = sem("acc_zero")
        dst_in = sem("dst_in")
        w_in = sem("w_in")
        x_at = [sem(f"x_at{i}") for i in range(RINGS)]
        prep = sem("prep")
        masked = sem("masked")
        local_tr = sem("local_tr")
        row_tr = sem("row_tr")
        local_ok = sem("local_ok")
        x_tr = sem("x_tr")
        xT_ok = sem("xT_ok")
        kv_mm = sem("kv_mm")
        kv_out = sem("kv_out")
        kv_stored = [sem(f"kv_stored{i}") for i in range(RINGS)]
        q_mm = sem("q_mm")
        q_hi = sem("q_hi")
        q_sub = sem("q_sub")
        q_mid = sem("q_mid")
        q_lo = sem("q_lo")
        q_odd = sem("q_odd")
        idx_in = [sem(f"idx_in{i}") for i in range(RINGS)]
        attr_in = [sem(f"attr_in{i}") for i in range(2)]
        kv_in = [sem(f"kv_in{i}") for i in range(RINGS)]
        go = sem("go")
        attr_tr = sem("attr_tr")
        attrT_ok = sem("attrT_ok")
        e_mm = sem("e_mm")
        hot_ok = sem("hot_ok")
        hot_tr = sem("hot_tr")
        hotT_ok = sem("hotT_ok")
        q_sel = sem("q_sel")
        ke = sem("ke")
        keq = sem("keq")
        dot = sem("dot")
        clip = sem("clip")
        exp_ok = sem("exp_ok")
        msg_ok = sem("msg_ok")
        sums = sem("sums")
        added = sem("added")
        stray_go = sem("stray_go")
        s_idx = sem("s_idx")
        s_attr = sem("s_attr")
        s_kv = sem("s_kv")
        s_tr = sem("s_tr")
        s_attrT = sem("s_attrT")
        s_e = sem("s_e")
        s_ke = sem("s_ke")
        s_cur = sem("s_cur")
        s_hot = sem("s_hot")
        s_hot_tr = sem("s_hot_tr")
        s_hotT = sem("s_hotT")
        s_q = sem("s_q")
        s_keq = sem("s_keq")
        s_dot = sem("s_dot")
        s_clip = sem("s_clip")
        s_exp = sem("s_exp")
        s_msg = sem("s_msg")
        s_sums = sem("s_sums")
        s_added = sem("s_added")
        all_added = sem("all_added")
        moved_zero = sem("moved_zero")
        moved_in = [sem(f"moved_in{c}") for c in range(FC)]
        total = sem("total")
        x_back = sem("x_back")
        zadd = sem("zadd")
        zrec = sem("zrec")
        attn = sem("attn")
        resid = sem("resid")
        stat = sem("stat")
        aggr = sem("aggr")
        std_ok = sem("std_ok")
        rstd_ok = sem("rstd_ok")
        shift_ok = sem("shift_ok")
        norm_ok = sem("norm_ok")
        stored = sem("stored")

        def chunk_groups(c):
            return min(P, G - c * P)

        def per_head(ap):
            return ap.rearrange("p t (h d) -> p t h d", h=HEADS)

        block = ctx.enter_context(nc.Block())

        @block.sync
        def _(sp):
            sp.wait_ge(rows_zero, 1)
            full = (GC - 1) * P
            sp.dma_start(dst_rows[:, 0:GC - 1, :],
                         dst[0:full * GROUP].rearrange("(c p e) -> p c e", p=P, e=GROUP)).then_inc(dst_in, 16)
            sp.dma_start(dst_rows[0:LAST_ROW, GC - 1, :],
                         dst[full * GROUP:(G - 1) * GROUP].rearrange("(p e) -> p e", e=GROUP)).then_inc(dst_in, 16)
            sp.dma_start(dst_rows[LAST_ROW:LAST_ROW + 1, GC - 1, :],
                         dst[n_edges - GROUP:n_edges].rearrange("(p e) -> p e", e=GROUP)).then_inc(dst_in, 16)

            def load_x(c):
                n = chunk_windows(c)
                if c >= RINGS and c < CH - 1:
                    sp.wait_ge(x_tr, c - RINGS + 1)
                if c < CH - 1:
                    sp.dma_start(x_in[:, c % RINGS, 0:n, :], x[c * CW * P:(c * CW + n) * P, :]
                                 .rearrange("(w p) d -> p w d", p=P)).then_inc(x_at[c % RINGS], 16)
                else:
                    sp.wait_ge(x_zero, 1)
                    sp.dma_start(x_last[0:LAST_NODES, :], x[(WIN - 1) * P:n_nodes, :]).then_inc(x_at[c % RINGS], 16)

            for c in range(RINGS):
                load_x(c)
            sp.dma_start(w_kv[:, 0:dim], wk).then_inc(w_in, 16)
            sp.dma_start(w_kv[:, dim:2 * dim], wv).then_inc(w_in, 16)
            sp.dma_start(w_q[:, :], wq).then_inc(w_in, 16)
            sp.dma_start(w_e[:, :], we).then_inc(w_in, 16)
            for c in range(CH):
                if c + RINGS < CH:
                    load_x(c + RINGS)
                n = chunk_windows(c)
                sp.wait_ge(kv_out, min(2 * (c + 1), -(-WIN // 2)))
                if c < CH - 1:
                    sp.dma_start(kv_table[c * CW * P:(c * CW + n) * P, :].rearrange("(w p) d -> p w d", p=P),
                                 kv[:, c % RINGS, 0:n, :]).then_inc(kv_stored[c % RINGS], 16)
                else:
                    sp.dma_start(kv_table[(WIN - 1) * P:n_nodes, :], kv[0:LAST_NODES, c % RINGS, 0, :])\
                        .then_inc(kv_stored[c % RINGS], 16)

            def load_group(b, u):
                g = b * RINGS + u
                if past(g, RINGS):
                    sp.wait_ge(kv_in[u], b * TILES * 16)
                sp.dma_start(src_idx[:, u, :], src[bass.ds(edge0(g), GROUP)].rearrange("(p t) -> p t", p=P)
                             .bitcast(U32)).then_inc(idx_in[u], 16)
                if past(g, 2):
                    sp.wait_ge(attr_tr, g - 1)
                sp.dma_start(attr[:, u % 2, :, :], edge_attr[bass.ds(edge0(g), GROUP), :]
                             .rearrange("(p t) d -> p t d", p=P)).then_inc(attr_in[u % 2], 16)

            load_group(0, 0)
            load_group(0, 1)
            for u in (2, 3):
                sp.dma_start(src_idx[:, u, :], src[u * GROUP:(u + 1) * GROUP].rearrange("(p t) -> p t", p=P)
                             .bitcast(U32)).then_inc(idx_in[u], 16)
            sp.wait_ge(local_ok, 1)
            for c in range(CH):
                w0, n = c * CW, chunk_windows(c)
                sp.wait_ge(q_lo, c + 1)
                up = min(w0 + n, ODD)
                if up > w0:
                    sp.dma_start(Qp[0:HALF, WIN + w0:WIN + up, :, :], Qp[HALF:P, w0:up, :, :]).then_inc(q_odd, 16)
                lo = max(w0, 1)
                sp.dma_start(Qp[HALF:P, WIN + lo - 1:WIN + w0 + n - 1, :, :], Qp[0:HALF, lo:w0 + n, :, :])\
                    .then_inc(q_odd, 16)
            for u in (2, 3):
                sp.wait_ge(attr_tr, u - 1)
                sp.dma_start(attr[:, u % 2, :, :], edge_attr[u * GROUP:(u + 1) * GROUP, :]
                             .rearrange("(p t) d -> p t d", p=P)).then_inc(attr_in[u % 2], 16)

            with sp.Fori(1, B_LAST) as b:
                for u in range(RINGS):
                    load_group(b, u)
            for g in range(B_LAST * RINGS, G):
                load_group(g // RINGS, g % RINGS)

            sp.wait_ge(local_ok, 1)
            sp.wait_ge(first_ok, 1)
            with sp.If(sp.value_load(table[0:1, 1, G:G + 1], min_val=0, max_val=G) > 0):
                with sp.Fori(0, G) as g:
                    nth = sp.value_load(table[0:1, 1, bass.ds(g, 1)], min_val=0, max_val=G)
                    nth_next = sp.value_load(table[0:1, 1, bass.ds(g + 1, 1)], min_val=0, max_val=G)
                    with sp.If(nth_next > nth):
                        first = sp.value_load(table[0:1, 2, bass.ds(g, 1)], min_val=0, max_val=n_edges - GROUP)
                        sp.wait_ge(s_added, nth * WIN + 1)
                        sp.sem_inc(stray_go, 1)
                        sp.dma_start(src_idx[:, 0, :], src[bass.ds(first, GROUP)]
                                     .rearrange("(p t) -> p t", p=P).bitcast(U32)).then_inc(s_idx, 16)
                        sp.dma_start(attr[:, 0, :, :], edge_attr[bass.ds(first, GROUP), :]
                                     .rearrange("(p t) d -> p t d", p=P)).then_inc(s_attr, 16)

            sp.wait_ge(all_added, 1)
            for c in range(FC):
                w0, w1 = c * FW, (c + 1) * FW
                up = min(w1, ODD)
                sp.dma_start(moved[HALF:P, w0:up, :], acc[0:HALF, WIN + w0:WIN + up, :]).then_inc(moved_in[c], 16)
                lo = max(w0, 1)
                sp.dma_start(moved[0:HALF, lo:w1, :], acc[HALF:P, WIN + lo - 1:WIN + w1 - 1, :])\
                    .then_inc(moved_in[c], 16)
            for c in range(FC):
                sp.wait_ge(norm_ok, c + 1)
                if c < FC - 1:
                    sp.dma_start(out[c * FW * P:(c + 1) * FW * P, :].rearrange("(w p) d -> p w d", p=P),
                                 normed[:, c * FW:(c + 1) * FW, :]).then_inc(stored, 16)
                else:
                    sp.dma_start(out[c * FW * P:(WIN - 1) * P, :].rearrange("(w p) d -> p w d", p=P),
                                 normed[:, c * FW:WIN - 1, :]).then_inc(stored, 16)
                    sp.dma_start(out[(WIN - 1) * P:n_nodes, :], normed[0:LAST_NODES, WIN - 1, :])\
                        .then_inc(stored, 16)
            sp.wait_ge(stored, 16 * (FC + 1))

        @block.gpsimd
        def _(pool):
            nc.gpsimd.memset(ident[:, :], 0.0).then_inc(id_zero, 1)
            nc.gpsimd.iota(iota[:, :], [[1, P]], base=0, channel_multiplier=0,
                           allow_small_or_imprecise_dtypes=True).then_inc(const_ready, 1)
            nc.gpsimd.iota(table[0:1, 2, 0:G - 1], [[GROUP, G - 1]], base=0, channel_multiplier=0)
            nc.gpsimd.iota(table[0:1, 2, G - 1:G], [[0, 1]], base=edge0(G - 1), channel_multiplier=0)\
                .then_inc(first_ok, 1)
            pool.wait_ge(id_zero, 1)
            nc.gpsimd.affine_select(out=ident[:, :], in_=ident[:, :], compare_op=ALU.not_equal, fill=1.0, base=0,
                                    pattern=[[-1, P]], channel_multiplier=1).then_inc(const_ready, 1)
            pool.wait_ge(prep, 6)
            last = local_rows[:, GC - 1, :]
            nc.gpsimd.affine_select(out=last, in_=last, compare_op=ALU.is_ge, fill=NOT_AN_EDGE,
                                    base=LAST_ROW * 2 * GROUP - REPEATED, pattern=[[1, GROUP]],
                                    channel_multiplier=-2 * GROUP).then_inc(masked, 1)
            nc.gpsimd.memset(acc[:, :, :], 0.0).then_inc(acc_zero, 1)

            def gather(b, u):
                g = b * RINGS + u
                pool.wait_ge(idx_in[u], b * 16 + 16)
                if past(g, RINGS):
                    pool.wait_ge(msg_ok, g - RINGS + 1)
                pool.sem_inc(go, 1)
                for t in range(TILES):
                    nc.gpsimd.indirect_dma_start(
                        out=kv[:, u, t, :], out_offset=None, in_=kv_table,
                        in_offset=bass.IndirectOffsetOnAxis(ap=src_idx[:, u, t:t + 1], axis=0)).then_inc(kv_in[u], 16)

            for i in range(RINGS):
                pool.wait_ge(kv_stored[i], 16 * len(range(i, CH, RINGS)))
            for u in range(RINGS):
                gather(0, u)
            with pool.Fori(1, B_LAST) as b:
                for u in range(RINGS):
                    gather(b, u)
            for g in range(B_LAST * RINGS, G):
                gather(g // RINGS, g % RINGS)

            pool.wait_ge(local_ok, 1)
            with pool.If(pool.value_load(table[0:1, 1, G:G + 1], min_val=0, max_val=G) > 0):
                with pool.Fori(0, G) as g:
                    nth = pool.value_load(table[0:1, 1, bass.ds(g, 1)], min_val=0, max_val=G)
                    nth_next = pool.value_load(table[0:1, 1, bass.ds(g + 1, 1)], min_val=0, max_val=G)
                    with pool.If(nth_next > nth):
                        pool.wait_ge(s_idx, nth * 16 + 16)
                        pool.sem_inc(go, 1)
                        for t in range(TILES):
                            nc.gpsimd.indirect_dma_start(
                                out=kv[:, 0, t, :], out_offset=None, in_=kv_table,
                                in_offset=bass.IndirectOffsetOnAxis(ap=src_idx[:, 0, t:t + 1], axis=0))\
                                .then_inc(s_kv, 16)

            pool.wait_ge(moved_zero, 1)
            for c in range(FC):
                pool.wait_ge(moved_in[c], 32)
                w = slice(c * FW, (c + 1) * FW)
                nc.gpsimd.tensor_tensor(acc[:, w, :], acc[:, w, :], moved[:, w, :], ALU.add).then_inc(total, 1)

        @block.tensor
        def _(pe):
            pe.wait_ge(const_ready, 2)
            pe.wait_ge(masked, 1)
            bank = [psE[:, 0, :], psE[:, 1, :], psQ[:, 0, :], psQ[:, 1, :]]
            for t in range(TILES):
                for c in range(GC):
                    edges = local_rows[:, c, :].rearrange("g (p t) -> g t p", t=TILES)[:, t, :]
                    last = nc.tensor.transpose(bank[t][:, c * P:(c + 1) * P], edges, ident[:, :])
            last.then_inc(local_tr, 1)
            pe.wait_ge(prep, 11)
            for c in range(GC):
                cols = slice(c * P, (c + 1) * P)
                nc.tensor.matmul(psW[0:1, 0, cols], slot_col[:, c:c + 1], ident[:, :], start=True, stop=True)
                nc.tensor.matmul(psW[0:1, 1, cols], stray_col[:, c:c + 1], ident[:, :], start=True, stop=True)
                last = nc.tensor.matmul(psH[:, cols], home_col[:, c:c + 1].to_broadcast([P, P]), ident[:, :],
                                        start=True, stop=True)
            last.then_inc(row_tr, 1)
            pe.wait_ge(local_ok, 1)
            pe.wait_ge(w_in, 64)

            def kv_products(c):
                pe.wait_ge(xT_ok, c + 1)
                for i in range(0, chunk_windows(c), 2):
                    pair = c * (CW // 2) + i // 2
                    if pair >= 4:
                        pe.wait_ge(kv_out, pair - 3)
                    for w in range(c * CW + i, min(c * CW + i + 2, WIN)):
                        o = (w % 2) * 2 * dim
                        last = nc.tensor.matmul(bank[pair % 4][:, o:o + 2 * dim], xT[:, w * P:(w + 1) * P],
                                                w_kv[:, :], start=True, stop=True)
                    last.then_inc(kv_mm, 1)

            for c in range(CH):
                pe.wait_ge(x_at[c % RINGS], 16 * (c // RINGS + 1))
                if c >= 2:
                    pe.wait_ge(xT_ok, c - 1)
                for i in range(chunk_windows(c)):
                    nodes = x_in[:, c % RINGS, i, :] if c < CH - 1 else x_last
                    last = nc.tensor.transpose(psX[c % 2][:, i * P:(i + 1) * P], nodes, ident[:, :])
                last.then_inc(x_tr, 1)
                if c >= 1:
                    kv_products(c - 1)
            kv_products(CH - 1)
            for c in range(CH):
                if c >= 2:
                    pe.wait_ge(q_sub, c - 1)
                for i in range(chunk_windows(c)):
                    w = c * CW + i
                    last = nc.tensor.matmul(psW[:, c % 2, i * P:(i + 1) * P], xT[:, w * P:(w + 1) * P], w_q[:, :],
                                            start=True, stop=True)
                last.then_inc(q_mm, 1)

            def turn_attr(b, u):
                g = b * RINGS + u
                pe.wait_ge(attr_in[u % 2], b * 32 + (u // 2) * 16 + 16)
                if past(g, 1):
                    pe.wait_ge(attrT_ok, g)
                for t in range(TILES):
                    last = nc.tensor.transpose(psT[:, t * P:(t + 1) * P], attr[:, u % 2, t, :], ident[:, :])
                last.then_inc(attr_tr, 1)

            def edge_products(b, u):
                g = b * RINGS + u
                pe.wait_ge(attrT_ok, g + 1)
                if past(g, 2):
                    pe.wait_ge(ke, g - 1)
                for t in range(TILES):
                    last = nc.tensor.matmul(psE[:, u % 2, t * P:(t + 1) * P], attrT[:, u % 2, t * P:(t + 1) * P],
                                            w_e[:, :], start=True, stop=True)
                last.then_inc(e_mm, 1)

            def turn_hot(b, u):
                g = b * RINGS + u
                pe.wait_ge(hot_ok, g + 1)
                if past(g, 1):
                    pe.wait_ge(hotT_ok, g)
                for t in range(TILES):
                    last = nc.tensor.transpose(psH[:, t * P:(t + 1) * P], hot[:, u, t, :], ident[:, :])
                last.then_inc(hot_tr, 1)

            def select_q(b, u):
                g = b * RINGS + u
                slot = pe.value_load(table[0:1, 0, bass.ds(g, 1)], min_val=0, max_val=SLOTS - 1)
                pe.wait_ge(hotT_ok, g + 1)
                if past(g, 2):
                    pe.wait_ge(keq, g - 1)
                for t in range(TILES):
                    for part in range(3):
                        last = nc.tensor.matmul(psQ[:, u % 2, t * P:(t + 1) * P], hotT[:, u % 2, t * P:(t + 1) * P],
                                                Qp[:, bass.ds(slot, 1), part, :].rearrange("p a d -> p (a d)"),
                                                start=(part == 0), stop=(part == 2))
                last.then_inc(q_sel, 1)

            def sum_messages(b, u):
                g = b * RINGS + u
                pe.wait_ge(msg_ok, g + 1)
                if past(g, 2):
                    pe.wait_ge(added, g - 1)
                for t in range(TILES):
                    last = nc.tensor.matmul(psW[:, u % 2, 0:MW], hot[:, u, t, :], msg[:, u % 2, t, :],
                                            start=(t == 0), stop=(t == TILES - 1))
                last.then_inc(sums, 1)

            def step(b, u):
                b1, u1 = b + (u + 1) // RINGS, (u + 1) % RINGS
                b2, u2 = b + (u + 2) // RINGS, (u + 2) % RINGS
                peeled = isinstance(b, int)
                if not peeled or b2 * RINGS + u2 < G:
                    turn_attr(b2, u2)
                if not peeled or b1 * RINGS + u1 < G:
                    edge_products(b1, u1)
                    select_q(b1, u1)
                if not peeled or b2 * RINGS + u2 < G:
                    turn_hot(b2, u2)
                sum_messages(b, u)

            pe.wait_ge(local_ok, 1)
            pe.wait_ge(q_lo, CH)
            pe.wait_ge(q_odd, 16 * q_odd_dmas)
            for u in range(2):
                turn_attr(0, u)
                turn_hot(0, u)
            edge_products(0, 0)
            select_q(0, 0)
            for u in range(RINGS):
                step(0, u)
            with pe.Fori(1, B_LAST) as b:
                for u in range(RINGS):
                    step(b, u)
            for g in range(B_LAST * RINGS, G):
                step(g // RINGS, g % RINGS)

            with pe.If(pe.value_load(table[0:1, 1, G:G + 1], min_val=0, max_val=G) > 0):
                with pe.Fori(0, G) as g:
                    nth = pe.value_load(table[0:1, 1, bass.ds(g, 1)], min_val=0, max_val=G)
                    nth_next = pe.value_load(table[0:1, 1, bass.ds(g + 1, 1)], min_val=0, max_val=G)
                    with pe.If(nth_next > nth):
                        pe.wait_ge(s_attr, nth * 16 + 16)
                        for t in range(TILES):
                            last = nc.tensor.transpose(psT[:, t * P:(t + 1) * P], attr[:, 0, t, :], ident[:, :])
                        last.then_inc(s_tr, 1)
                        pe.wait_ge(s_attrT, nth + 1)
                        for t in range(TILES):
                            last = nc.tensor.matmul(psE[:, 0, t * P:(t + 1) * P], attrT[:, 0, t * P:(t + 1) * P],
                                                    w_e[:, :], start=True, stop=True)
                        last.then_inc(s_e, 1)
                        with pe.Fori(0, WIN) as w:
                            k = nth * WIN + w + 1
                            pe.wait_ge(s_hot, k)
                            for t in range(TILES):
                                last = nc.tensor.transpose(psH[:, t * P:(t + 1) * P], hot[:, 0, t, :], ident[:, :])
                            last.then_inc(s_hot_tr, 1)
                            pe.wait_ge(s_hotT, k)
                            for t in range(TILES):
                                for part in range(3):
                                    last = nc.tensor.matmul(
                                        psQ[:, 0, t * P:(t + 1) * P], hotT[:, 0, t * P:(t + 1) * P],
                                        Qp[:, bass.ds(w, 1), part, :].rearrange("p a d -> p (a d)"),
                                        start=(part == 0), stop=(part == 2))
                            last.then_inc(s_q, 1)
                            pe.wait_ge(s_msg, k)
                            for t in range(TILES):
                                last = nc.tensor.matmul(psW[:, 0, 0:MW], hot[:, 0, t, :], msg[:, 0, t, :],
                                                        start=(t == 0), stop=(t == TILES - 1))
                            last.then_inc(s_sums, 1)

            pe.wait_ge(all_added, 1)
            for c in range(FC):
                if c >= 2:
                    pe.wait_ge(resid, c - 1)
                for i in range(FW):
                    w = c * FW + i
                    to = (psE if i < 4 else psQ)[:, c % 2, (i % 4) * P:(i % 4 + 1) * P]
                    last = nc.tensor.transpose(to, xT[:, w * P:(w + 1) * P], ident[:, :])
                last.then_inc(x_back, 1)

        @block.scalar
        def _(act):
            for c in range(CH):
                n = chunk_windows(c) * P
                act.wait_ge(x_tr, c + 1)
                nc.scalar.activation(xT[:, c * CW * P:c * CW * P + n], psX[c % 2][:, 0:n], ACT.Copy).then_inc(xT_ok, 1)

            def q_view(c, part):
                return Qp[:, c * CW:c * CW + chunk_windows(c), part, :]

            def first_part(c):
                act.wait_ge(q_mm, c + 1)
                n = chunk_windows(c)
                nc.scalar.activation(q_view(c, 0), psW[:, c % 2, 0:n * P].rearrange("p (w d) -> p w d", d=dim),
                                     ACT.Copy).then_inc(q_hi, 1)

            def second_part(c):
                act.wait_ge(q_sub, c + 1)
                n = chunk_windows(c)
                nc.scalar.activation(q_view(c, 1), q_rest[:, c % 2, 0:n * P].rearrange("p (w d) -> p w d", d=dim),
                                     ACT.Copy).then_inc(q_mid, 1)

            first_part(0)
            for c in range(CH):
                if c + 1 < CH:
                    first_part(c + 1)
                second_part(c)
            act.wait_ge(q_lo, CH)

            def copy_attr(b, u):
                g = b * RINGS + u
                act.wait_ge(attr_tr, g + 1)
                if past(g, 2):
                    act.wait_ge(e_mm, g - 1)
                nc.scalar.activation(attrT[:, u % 2, :], psT[:, :], ACT.Copy).then_inc(attrT_ok, 1)

            def copy_hot(b, u):
                g = b * RINGS + u
                act.wait_ge(hot_tr, g + 1)
                if past(g, 2):
                    act.wait_ge(q_sel, g - 1)
                nc.scalar.activation(hotT[:, u % 2, :], psH[:, :], ACT.Copy).then_inc(hotT_ok, 1)

            def exponentials(b, u):
                g = b * RINGS + u
                act.wait_ge(clip, g + 1)
                if past(g, 2):
                    act.wait_ge(sums, g - 1)
                nc.scalar.activation(msg[:, u % 2, :, dim:MW], clipped[:, :].rearrange("p (t h) -> p t h", h=HEADS),
                                     ACT.Exp, scale=SCALE).then_inc(exp_ok, 1)

            def step(b, u):
                b2, u2 = b + (u + 2) // RINGS, (u + 2) % RINGS
                ahead = not isinstance(b, int) or b2 * RINGS + u2 < G
                if ahead:
                    copy_attr(b2, u2)
                exponentials(b, u)
                if ahead:
                    copy_hot(b2, u2)

            for u in range(2):
                copy_attr(0, u)
                copy_hot(0, u)
            for u in range(RINGS):
                step(0, u)
            with act.Fori(1, B_LAST) as b:
                for u in range(RINGS):
                    step(b, u)
            for g in range(B_LAST * RINGS, G):
                step(g // RINGS, g % RINGS)

            act.wait_ge(local_ok, 1)
            with act.If(act.value_load(table[0:1, 1, G:G + 1], min_val=0, max_val=G) > 0):
                with act.Fori(0, G) as g:
                    nth = act.value_load(table[0:1, 1, bass.ds(g, 1)], min_val=0, max_val=G)
                    nth_next = act.value_load(table[0:1, 1, bass.ds(g + 1, 1)], min_val=0, max_val=G)
                    with act.If(nth_next > nth):
                        act.wait_ge(s_tr, nth + 1)
                        nc.scalar.activation(attrT[:, 0, :], psT[:, :], ACT.Copy).then_inc(s_attrT, 1)
                        with act.Fori(0, WIN) as w:
                            k = nth * WIN + w + 1
                            act.wait_ge(s_hot_tr, k)
                            nc.scalar.activation(hotT[:, 0, :], psH[:, :], ACT.Copy).then_inc(s_hotT, 1)
                            act.wait_ge(s_clip, k)
                            nc.scalar.activation(msg[:, 0, :, dim:MW],
                                                 clipped[:, :].rearrange("p (t h) -> p t h", h=HEADS),
                                                 ACT.Exp, scale=SCALE).then_inc(s_exp, 1)

            for c in range(FC):
                act.wait_ge(aggr, c + 1)
                nc.scalar.activation(std[:, c % 2, :], mean_var[:, c % 2, :, 1], ACT.Sqrt, bias=ln_eps[:, 0:1])\
                    .then_inc(std_ok, 1)
                act.wait_ge(shift_ok, c + 1)
                for i in range(FW):
                    w = c * FW + i
                    last = nc.scalar.activation(normed[:, w, :], acc[:, w, 0:dim], ACT.Identity,
                                                bias=shift[:, c % 2, i:i + 1], scale=rstd[:, c % 2, i:i + 1])
                last.then_inc(norm_ok, 1)

        @block.vector
        def _(dve):
            nc.vector.memset(dst_rows, 0).then_inc(rows_zero, 1)
            nc.vector.memset(x_last[LAST_NODES // 32 * 32:P, :], 0.0).then_inc(x_zero, 1)
            nc.vector.memset(ln_eps[:, :], LN_EPS)
            dve.wait_ge(dst_in, 48)
            nc.vector.tensor_scalar(hcol[:, :], dst_rows[:, :, 0], 6, None, ALU.logical_shift_right).then_inc(prep, 1)
            dve.wait_ge(prep, 1)
            nc.vector.tensor_scalar(hcol[:, :], hcol[:, :], 2 * (WIN - 1), None, ALU.min).then_inc(prep, 1)
            dve.wait_ge(prep, 2)
            nc.vector.tensor_scalar(home_col[:, :], hcol[:, :], float(HALF), None, ALU.mult).then_inc(prep, 1)
            nc.vector.tensor_scalar(odd_col[:, :], hcol[:, :], 1, None, ALU.bitwise_and)
            nc.vector.tensor_scalar(pair_col[:, :], hcol[:, :], 1, None, ALU.logical_shift_right).then_inc(prep, 1)
            dve.wait_ge(prep, 4)
            nc.vector.scalar_tensor_tensor(slot_col[:, :], odd_col[:, :], float(WIN), pair_col[:, :],
                                           ALU.mult, ALU.add).then_inc(prep, 1)
            for c in range(GC):
                last = nc.vector.tensor_scalar(local_rows[:, c, :], dst_rows[:, c, :], home_col[:, c:c + 1], None,
                                               ALU.subtract)
            last.then_inc(prep, 1)
            dve.wait_ge(prep, 6)
            dve.wait_ge(masked, 1)
            nc.vector.tensor_reduce(least[:, :], local_rows, AX.X, ALU.min).then_inc(prep, 1)
            nc.vector.tensor_reduce(most[:, :], local_rows, AX.X, ALU.max).then_inc(prep, 1)
            dve.wait_ge(prep, 8)
            nc.vector.tensor_scalar(least[:, :], least[:, :], 0.0, None, ALU.is_lt).then_inc(prep, 1)
            nc.vector.tensor_scalar(most[:, :], most[:, :], float(P - 1), None, ALU.is_gt).then_inc(prep, 1)
            dve.wait_ge(prep, 10)
            nc.vector.tensor_tensor(stray_col[:, :], least[:, :], most[:, :], ALU.max).then_inc(prep, 1)
            dve.wait_ge(local_tr, 1)
            bank = [psE[:, 0, :], psE[:, 1, :], psQ[:, 0, :], psQ[:, 1, :]]
            for t in range(TILES):
                nc.vector.tensor_copy(local[:, t, :], bank[t][:, 0:G])
            dve.wait_ge(row_tr, 1)
            nc.vector.tensor_copy(home[:, :], psH[:, :])
            nc.vector.tensor_copy(table[0:1, 0, 0:G], psW[0:1, 0, 0:G])
            nc.vector.tensor_copy(stray_row[0:1, :], psW[0:1, 1, 0:G]).then_inc(prep, 1)
            dve.wait_ge(prep, 12)
            nc.vector.tensor_tensor_scan(stray_sum[0:1, :], stray_row[0:1, :], stray_row[0:1, :], 0.0,
                                         ALU.add, ALU.bypass).then_inc(prep, 1)
            dve.wait_ge(prep, 13)
            nc.vector.memset(table[0:1, 1, 0:1], 0)
            nc.vector.tensor_copy(table[0:1, 1, 1:G + 1], stray_sum[0:1, :]).then_inc(local_ok, 1)


            for pair in range(-(-WIN // 2)):
                c, o = pair // (CW // 2), pair % (CW // 2) * 2
                n = min(2, WIN - 2 * pair)
                dve.wait_ge(kv_mm, pair + 1)
                if c >= RINGS and o == 0:
                    dve.wait_ge(kv_stored[c % RINGS], c // RINGS * 16)
                nc.vector.tensor_copy(kv[:, c % RINGS, o:o + n, :],
                                      bank[pair % 4][:, 0:n * 2 * dim].rearrange("p (w d) -> p w d", w=n))\
                    .then_inc(kv_out, 1)

            def q_view(c, part):
                return Qp[:, c * CW:c * CW + chunk_windows(c), part, :]

            def rest_view(c):
                return q_rest[:, c % 2, 0:chunk_windows(c) * P].rearrange("p (w d) -> p w d", d=dim)

            def after_first(c):
                dve.wait_ge(q_hi, c + 1)
                if c >= 2:
                    dve.wait_ge(q_lo, c - 1)
                full = psW[:, c % 2, 0:chunk_windows(c) * P].rearrange("p (w d) -> p w d", d=dim)
                nc.vector.tensor_tensor(rest_view(c), full, q_view(c, 0), ALU.subtract).then_inc(q_sub, 1)

            def third_part(c):
                dve.wait_ge(q_mid, c + 1)
                nc.vector.tensor_tensor(q_view(c, 2), rest_view(c), q_view(c, 1), ALU.subtract).then_inc(q_lo, 1)

            after_first(0)
            for c in range(CH):
                if c + 1 < CH:
                    after_first(c + 1)
                third_part(c)

            def mark(b, u):
                g = b * RINGS + u
                if past(g, RINGS):
                    dve.wait_ge(sums, g - RINGS + 1)
                for t in range(TILES):
                    last = nc.vector.tensor_scalar(hot[:, u, t, :], iota[:, :], local[:, t, bass.ds(g, 1)], None,
                                                   ALU.is_equal)
                last.then_inc(hot_ok, 1)

            def scores(b, u):
                g = b * RINGS + u
                dve.wait_ge(e_mm, g + 1)
                dve.wait_ge(kv_in[u], b * TILES * 16 + TILES * 16)
                tiles = prod[:, :].rearrange("p (t d) -> p t d", d=dim)
                nc.vector.tensor_tensor(tiles, kv[:, u, :, 0:dim],
                                        psE[:, u % 2, :].rearrange("p (t d) -> p t d", d=dim), ALU.mult).then_inc(ke, 1)
                dve.wait_ge(ke, g + 1)
                dve.wait_ge(q_sel, g + 1)
                nc.vector.tensor_tensor(prod[:, :], prod[:, :], psQ[:, u % 2, :], ALU.mult).then_inc(keq, 1)
                dve.wait_ge(keq, g + 1)
                if past(g, 1):
                    dve.wait_ge(clip, g)
                nc.vector.tensor_reduce(score[:, :], prod[:, :].rearrange("p (a d) -> p a d", d=DH), AX.X, ALU.add)\
                    .then_inc(dot, 1)
                dve.wait_ge(dot, g + 1)
                if past(g, 1):
                    dve.wait_ge(exp_ok, g)
                nc.vector.tensor_scalar(clipped[:, :], score[:, :], SCORE_LIMIT / SCALE, -SCORE_LIMIT / SCALE,
                                        ALU.min, ALU.max).then_inc(clip, 1)

            def messages(b, u):
                g = b * RINGS + u
                dve.wait_ge(exp_ok, g + 1)
                nc.vector.tensor_tensor(per_head(msg[:, u % 2, :, 0:dim]), per_head(kv[:, u, :, dim:2 * dim]),
                                        msg[:, u % 2, :, dim:MW].unsqueeze(3).to_broadcast([P, TILES, HEADS, DH]),
                                        ALU.mult).then_inc(msg_ok, 1)

            def add_sums(b, u):
                g = b * RINGS + u
                slot = dve.value_load(table[0:1, 0, bass.ds(g, 1)], min_val=0, max_val=SLOTS - 1)
                dve.wait_ge(sums, g + 1)
                if past(g, 1):
                    dve.wait_ge(added, g)
                where = acc[:, bass.ds(slot, 1), :].rearrange("p a m -> p (a m)")
                nc.vector.tensor_tensor(where, psW[:, u % 2, 0:MW], where, ALU.add).then_inc(added, 1)

            def step(b, u):
                b0, u0 = b + (u - 1) // RINGS, (u - 1) % RINGS
                b2, u2 = b + (u + 2) // RINGS, (u + 2) % RINGS
                scores(b, u)
                if not isinstance(b, int) or b2 * RINGS + u2 < G:
                    mark(b2, u2)
                messages(b, u)
                if not isinstance(b, int) or b0 >= 0:
                    add_sums(b0, u0)

            dve.wait_ge(acc_zero, 1)
            for u in range(2):
                mark(0, u)
            for u in range(RINGS):
                step(0, u)
            with dve.Fori(1, B_LAST) as b:
                for u in range(RINGS):
                    step(b, u)
            for g in range(B_LAST * RINGS, G):
                step(g // RINGS, g % RINGS)
            add_sums((G - 1) // RINGS, (G - 1) % RINGS)
            dve.wait_ge(added, G)
            nc.vector.memset(cur[:, :, :], BIG).then_inc(s_added, 1)

            with dve.If(dve.value_load(table[0:1, 1, G:G + 1], min_val=0, max_val=G) > 0):
                with dve.Fori(0, G) as g:
                    nth = dve.value_load(table[0:1, 1, bass.ds(g, 1)], min_val=0, max_val=G)
                    nth_next = dve.value_load(table[0:1, 1, bass.ds(g + 1, 1)], min_val=0, max_val=G)
                    with dve.If(nth_next > nth):
                        dve.wait_ge(s_added, nth * WIN + 1)
                        where = local[:, :, bass.ds(g, 1)].rearrange("p t a -> p (t a)")
                        c0 = nth * 4 + 1
                        nc.vector.tensor_scalar(cur[:, 0, :], where, 0.0, None, ALU.is_ge)
                        nc.vector.tensor_scalar(cur[:, 1, :], where, float(P - 1), BIG, ALU.is_le, ALU.mult)\
                            .then_inc(s_cur, 1)
                        dve.wait_ge(s_cur, c0)
                        nc.vector.tensor_tensor(cur[:, 1, :], cur[:, 1, :], cur[:, 0, :], ALU.mult).then_inc(s_cur, 1)
                        dve.wait_ge(s_cur, c0 + 1)
                        nc.vector.tensor_tensor(cur[:, 0, :], cur[:, 1, :], where, ALU.add).then_inc(s_cur, 1)
                        dve.wait_ge(s_cur, c0 + 2)
                        nc.vector.tensor_scalar(cur[:, 0, :], cur[:, 0, :], home[:, bass.ds(g, 1)], None, ALU.add)\
                            .then_inc(s_cur, 1)
                        dve.wait_ge(s_e, nth + 1)
                        dve.wait_ge(s_kv, nth * (TILES * 16) + TILES * 16)
                        nc.vector.tensor_tensor(prod[:, :].rearrange("p (t d) -> p t d", d=dim), kv[:, 0, :, 0:dim],
                                                psE[:, 0, :].rearrange("p (t d) -> p t d", d=dim), ALU.mult)\
                            .then_inc(s_ke, 1)
                        keq_w = hot[:, 1, :, :].rearrange("p t d -> p (t d)")
                        with dve.Fori(0, WIN) as w:
                            k = nth * WIN + w + 1
                            dve.wait_ge(s_cur, c0 + 3)
                            for t in range(TILES):
                                last = nc.vector.tensor_scalar(hot[:, 0, t, :], iota[:, :], cur[:, 0, t:t + 1], None,
                                                               ALU.is_equal)
                            last.then_inc(s_hot, 1)
                            dve.wait_ge(s_ke, nth + 1)
                            dve.wait_ge(s_q, k)
                            nc.vector.tensor_tensor(keq_w, prod[:, :], psQ[:, 0, :], ALU.mult).then_inc(s_keq, 1)
                            dve.wait_ge(s_keq, k)
                            nc.vector.tensor_reduce(score[:, :], keq_w.rearrange("p (a d) -> p a d", d=DH), AX.X,
                                                    ALU.add).then_inc(s_dot, 1)
                            dve.wait_ge(s_dot, k)
                            nc.vector.tensor_scalar(clipped[:, :], score[:, :], SCORE_LIMIT / SCALE,
                                                    -SCORE_LIMIT / SCALE, ALU.min, ALU.max).then_inc(s_clip, 1)
                            dve.wait_ge(s_exp, k)
                            nc.vector.tensor_tensor(
                                per_head(msg[:, 0, :, 0:dim]), per_head(kv[:, 0, :, dim:2 * dim]),
                                msg[:, 0, :, dim:MW].unsqueeze(3).to_broadcast([P, TILES, HEADS, DH]), ALU.mult)\
                                .then_inc(s_msg, 1)
                            dve.wait_ge(s_sums, k)
                            at = acc[:, bass.ds(w, 1), :].rearrange("p a m -> p (a m)")
                            nc.vector.tensor_scalar(cur[:, 0, :], cur[:, 0, :], float(P), None, ALU.subtract)
                            nc.vector.tensor_tensor(at, psW[:, 0, 0:MW], at, ALU.add).then_inc(s_added, 1)
                            dve.wait_ge(s_added, k + 1)

            nc.vector.memset(moved[0:HALF, 0, :], 0.0)
            nc.vector.memset(moved[HALF:P, WIN - 1, :], 0.0).then_inc(moved_zero, 1)
            dve.wait_ge(moved_zero, 1)
            nc.vector.memset(score[:, :], 0.0).then_inc(all_added, 1)

            def scale_and_shift(c):
                dve.wait_ge(std_ok, c + 1)
                if c >= 2:
                    dve.wait_ge(norm_ok, c - 1)
                nc.vector.reciprocal(rstd[:, c % 2, :], std[:, c % 2, :]).then_inc(rstd_ok, 1)
                dve.wait_ge(rstd_ok, c + 1)
                nc.vector.scalar_tensor_tensor(shift[:, c % 2, :], mean_var[:, c % 2, :, 0], -1.0, rstd[:, c % 2, :],
                                               ALU.mult, ALU.mult).then_inc(shift_ok, 1)

            for c in range(FC):
                w = slice(c * FW, (c + 1) * FW)
                dve.wait_ge(total, c + 1)
                nc.vector.tensor_scalar(zinv[:, :, :], acc[:, w, dim:MW], Z_EPS, None, ALU.add).then_inc(zadd, 1)
                dve.wait_ge(zadd, c + 1)
                nc.vector.reciprocal(zinv[:, :, :], zinv[:, :, :]).then_inc(zrec, 1)
                dve.wait_ge(zrec, c + 1)
                nc.vector.tensor_tensor(per_head(acc[:, w, 0:dim]), per_head(acc[:, w, 0:dim]),
                                        zinv[:, :, :].unsqueeze(3).to_broadcast([P, FW, HEADS, DH]), ALU.mult)\
                    .then_inc(attn, 1)
                dve.wait_ge(attn, c + 1)
                dve.wait_ge(x_back, c + 1)
                for ps, w0, w1 in ((psE, c * FW, c * FW + 4), (psQ, c * FW + 4, (c + 1) * FW)):
                    last = nc.vector.tensor_tensor(
                        acc[:, w0:w1, 0:dim], acc[:, w0:w1, 0:dim],
                        ps[:, c % 2, 0:(w1 - w0) * dim].rearrange("p (w d) -> p w d", d=dim), ALU.add)
                last.then_inc(resid, 1)
                dve.wait_ge(resid, c + 1)
                for i in range(FW):
                    last = nc.vector.bn_stats(stats[:, i, :], acc[:, c * FW + i, 0:dim])
                last.then_inc(stat, 1)
                dve.wait_ge(stat, c + 1)
                if c >= 2:
                    dve.wait_ge(std_ok, c - 1)
                for i in range(FW):
                    last = nc.vector.bn_aggr(mean_var[:, c % 2, i, :], stats[:, i, :])
                last.then_inc(aggr, 1)
                if c >= 1:
                    scale_and_shift(c - 1)
            scale_and_shift(FC - 1)


_INS = ["x", "src", "dst", "edge_attr_128", "L0_gnn_WQ", "L0_gnn_WK", "L0_gnn_WV", "L0_gnn_WE"]
_OUT = ((6250, 128), "float32")


def kernel(**inputs):
    import numpy as _np
    import concourse.bacc as _bacc
    from concourse import mybir as _mybir
    from concourse.bass_utils import run_bass_kernel_spmd as _run

    nc = _bacc.Bacc("TRN2", target_bir_lowering=False, num_devices=1)
    arrays, args = {}, []
    for name in _INS:
        a = _np.ascontiguousarray(inputs[name])
        arrays[f"in_{name}_dram"] = a
        args.append(nc.dram_tensor(f"in_{name}_dram", a.shape, _mybir.dt.from_np(a.dtype), kind="ExternalInput").ap())
    args.append(nc.dram_tensor("out_0_dram", _OUT[0], _mybir.dt.from_np(_np.dtype(_OUT[1])), kind="ExternalOutput").ap())
    graph_attention_layernorm(nc, *args)
    r = _run(nc, [arrays], core_ids=[0])
    return r.results[0]["out_0_dram"]
```

```python
from contextlib import ExitStack

import concourse.bass as bass
from concourse import mybir

P = 128
F32 = mybir.dt.float32
BF16 = mybir.dt.bfloat16
I32 = mybir.dt.int32
U32 = mybir.dt.uint32
ALU = mybir.AluOpType
ACT = mybir.ActivationFunctionType
AX = mybir.AxisListType

HEADS = 8
RINGS = 4
BIG = 1.0e6
NOT_AN_EDGE = 0.5
SCORE_LIMIT = 5.0
Z_EPS = 1e-6
LN_EPS = 1e-5


def past(g, n):
    return g >= n if isinstance(g, int) else True


def graph_attention_layernorm(nc, x, src, dst, edge_attr, wq, wk, wv, we, out):
    n_nodes, dim = x.shape
    n_edges = src.shape[0]
    TILES = 4
    GROUP = TILES * P
    G = -(-n_edges // GROUP)
    REPEATED = G * GROUP - n_edges
    GC = -(-G // P)
    LAST_ROW = (G - 1) % P
    WIN = -(-n_nodes // P)
    ODD = WIN - 1
    SLOTS = WIN + ODD
    LAST_NODES = n_nodes - (WIN - 1) * P
    DH = dim // HEADS
    MW = dim + HEADS
    SCALE = float(DH) ** -0.5
    assert dim == P and SCALE == 0.25
    CW = 4
    CH = -(-WIN // CW)
    HALF = P // 2
    FW = 7
    FC = WIN // FW
    assert FC * FW == WIN
    B_LAST = G // RINGS

    def chunk_windows(c):
        return min(CW, WIN - c * CW)

    EARLY = CH // 2
    PREP = EARLY + 1
    q_odd_dmas = sum((c * CW < ODD) + 1 for c in range(CH))

    def edge0(g):
        return min(g * GROUP, n_edges - GROUP) if isinstance(g, int) else g * GROUP

    kv_table = nc.dram_tensor("kv_table", [n_nodes, 2 * dim], F32).ap()

    with ExitStack() as ctx:
        def sb(name, shape, dt=F32):
            return ctx.enter_context(nc.sbuf_tensor(name, shape, dt))

        def pb(name, shape):
            return ctx.enter_context(nc.psum_tensor(name, shape, F32))

        def sem(name):
            return ctx.enter_context(nc.semaphore(name))

        xT = sb("xT", [P, WIN * P])
        acc = sb("acc", [P, SLOTS, MW])
        Qp = sb("Qp", [P, SLOTS, 3, dim], BF16)
        kv = sb("kv", [P, RINGS, TILES, 2 * dim])
        src_idx = sb("src_idx", [P, RINGS, TILES], U32)
        attr = sb("attr", [P, 2, TILES, dim])
        attrT = sb("attrT", [P, 2, GROUP])
        hot = sb("hot", [P, RINGS, TILES, P])
        hotT = sb("hotT", [P, 2, GROUP], BF16)
        prod = sb("prod", [P, GROUP])
        msg = sb("msg", [P, 2, TILES, MW])
        score = sb("score", [P, TILES * HEADS])
        clipped = sb("clipped", [P, TILES * HEADS])
        local = sb("local", [P, TILES, G])
        home = sb("home", [P, GC * P])
        table = sb("table", [1, 3, G + 1], I32)
        iota = sb("iota", [P, P])
        ident = sb("ident", [P, P])
        w_kv = sb("w_kv", [P, 2 * dim])
        w_q = sb("w_q", [P, dim])
        w_e = sb("w_e", [P, dim])
        hcol = sb("hcol", [P, GC], I32)
        odd_col = sb("odd_col", [P, GC], I32)
        pair_col = sb("pair_col", [P, GC], I32)
        home_col = sb("home_col", [P, GC])
        slot_col = sb("slot_col", [P, GC])
        stray = sb("stray", [P, G], BF16)
        ones_col = sb("ones_col", [P, 1], BF16)
        one = sb("one", [P, 1])
        cur = sb("cur", [P, 2, TILES])
        zinv = sb("zinv", [P, FW, HEADS])
        stats = sb("stats", [P, FW, 6])
        mean_var = sb("mean_var", [P, 2, FW, 2])
        std = sb("std", [P, 2, FW])
        rstd = sb("rstd", [P, 2, FW])
        shift = sb("shift", [P, 2, FW])
        ln_eps = sb("ln_eps", [P, 1])
        x_in = hot[:, :, :, :]
        x_last = prod[:, 0:dim]
        q_rest = attrT[:, :, :]
        least = msg[:, 0, :, :].rearrange("p t m -> p (t m)")[:, 0:G]
        most = msg[:, 1, :, :].rearrange("p t m -> p (t m)")[:, 0:G]
        stray_row = most[0:1, :]
        x_res = xT[:, :].rearrange("p (w d) -> p w d", d=dim)
        rows = Qp[:, :, :, :].rearrange("p s t d -> p (s t d)").bitcast(F32)[:, SLOTS * 3 * dim // 2 - GC * GROUP:]
        dst_rows = rows.bitcast(I32).rearrange("p (c e) -> p c e", c=GC)
        local_rows = rows.rearrange("p (c e) -> p c e", c=GC)
        moved = Qp[:, :, :, :].rearrange("p s t d -> p (s t d)").bitcast(F32)[:, 0:WIN * MW]\
            .rearrange("p (w m) -> p w m", m=MW)
        psT = pb("psT", [P, GROUP])
        psH = pb("psH", [P, GROUP])
        psE = pb("psE", [P, 2, GROUP])
        psQ = pb("psQ", [P, 2, GROUP])
        psW = pb("psW", [P, 2, GROUP])
        psX = [psT, psH]

        rows_zero = sem("rows_zero")
        x_zero = sem("x_zero")
        id_zero = sem("id_zero")
        const_ready = sem("const_ready")
        first_ok = sem("first_ok")
        acc_zero = sem("acc_zero")
        dst_in = sem("dst_in")
        w_in = sem("w_in")
        x_at = [sem(f"x_at{i}") for i in range(RINGS)]
        prep = sem("prep")
        masked = sem("masked")
        turned = sem("turned")
        unturned = sem("unturned")
        slots_ok = sem("slots_ok")
        x_tr = sem("x_tr")
        xT_ok = sem("xT_ok")
        kv_mm = sem("kv_mm")
        kv_out = sem("kv_out")
        kv_stored = [sem(f"kv_stored{i}") for i in range(RINGS)]
        q_mm = sem("q_mm")
        q_hi = sem("q_hi")
        q_sub = sem("q_sub")
        q_mid = sem("q_mid")
        q_lo = sem("q_lo")
        q_odd = sem("q_odd")
        x_pad = sem("x_pad")
        x_res_in = sem("x_res_in")
        range_ok = sem("range_ok")
        stray_ok = sem("stray_ok")
        stray_mm = sem("stray_mm")
        count = sem("count")
        table_ok = sem("table_ok")
        idx_in = [sem(f"idx_in{i}") for i in range(RINGS)]
        attr_in = [sem(f"attr_in{i}") for i in range(2)]
        kv_in = [sem(f"kv_in{i}") for i in range(RINGS)]
        go = sem("go")
        attr_tr = sem("attr_tr")
        attrT_ok = sem("attrT_ok")
        e_mm = sem("e_mm")
        apart = sem("apart")
        hot_ok = sem("hot_ok")
        hot_tr = sem("hot_tr")
        hotT_ok = sem("hotT_ok")
        q_sel = sem("q_sel")
        ke = sem("ke")
        keq = sem("keq")
        dot = sem("dot")
        clip = sem("clip")
        exp_ok = sem("exp_ok")
        msg_ok = sem("msg_ok")
        sums = sem("sums")
        added = sem("added")
        stray_go = sem("stray_go")
        s_idx = sem("s_idx")
        s_attr = sem("s_attr")
        s_kv = sem("s_kv")
        s_tr = sem("s_tr")
        s_attrT = sem("s_attrT")
        s_e = sem("s_e")
        s_ke = sem("s_ke")
        s_cur = sem("s_cur")
        s_hot = sem("s_hot")
        s_hot_tr = sem("s_hot_tr")
        s_hotT = sem("s_hotT")
        s_q = sem("s_q")
        s_keq = sem("s_keq")
        s_dot = sem("s_dot")
        s_clip = sem("s_clip")
        s_exp = sem("s_exp")
        s_msg = sem("s_msg")
        s_sums = sem("s_sums")
        s_added = sem("s_added")
        all_added = sem("all_added")
        moved_zero = sem("moved_zero")
        moved_in = [sem(f"moved_in{c}") for c in range(FC)]
        total = sem("total")
        zadd = sem("zadd")
        zrec = sem("zrec")
        attn = sem("attn")
        resid = sem("resid")
        stat = sem("stat")
        aggr = sem("aggr")
        std_ok = sem("std_ok")
        rstd_ok = sem("rstd_ok")
        shift_ok = sem("shift_ok")
        norm_ok = sem("norm_ok")
        stored = sem("stored")

        def chunk_groups(c):
            return min(P, G - c * P)

        def per_head(ap):
            return ap.rearrange("p t (h d) -> p t h d", h=HEADS)

        block = ctx.enter_context(nc.Block())

        @block.sync
        def _(sp):
            def load_x(c):
                n = chunk_windows(c)
                if c < CH - 1:
                    if c >= RINGS:
                        sp.wait_ge(x_tr, c - RINGS + 1)
                    sp.dma_start(x_in[:, c % RINGS, 0:n, :], x[c * CW * P:(c * CW + n) * P, :]
                                 .rearrange("(w p) d -> p w d", p=P)).then_inc(x_at[c % RINGS], 16)
                else:
                    sp.wait_ge(x_zero, 1)
                    sp.dma_start(x_last[0:LAST_NODES, :], x[(WIN - 1) * P:n_nodes, :]).then_inc(x_at[c % RINGS], 16)

            def load_index(b, u):
                g = b * RINGS + u
                if past(g, RINGS):
                    sp.wait_ge(kv_in[u], b * TILES * 16)
                sp.dma_start(src_idx[:, u, :], src[bass.ds(edge0(g), GROUP)].rearrange("(p t) -> p t", p=P)
                             .bitcast(U32)).then_inc(idx_in[u], 16)

            def load_attr(b, u):
                g = b * RINGS + u
                if past(g, 2):
                    sp.wait_ge(attr_tr, g - 1)
                sp.dma_start(attr[:, u % 2, :, :], edge_attr[bass.ds(edge0(g), GROUP), :]
                             .rearrange("(p t) d -> p t d", p=P)).then_inc(attr_in[u % 2], 16)

            for c in range(RINGS):
                load_x(c)
            full = (GC - 1) * P
            sp.dma_start(dst_rows[:, 0:GC - 1, :],
                         dst[0:full * GROUP].rearrange("(c p e) -> p c e", p=P, e=GROUP)).then_inc(dst_in, 16)
            sp.wait_ge(rows_zero, 1)
            sp.dma_start(dst_rows[0:LAST_ROW, GC - 1, :],
                         dst[full * GROUP:(G - 1) * GROUP].rearrange("(p e) -> p e", e=GROUP)).then_inc(dst_in, 16)
            sp.dma_start(dst_rows[LAST_ROW:LAST_ROW + 1, GC - 1, :],
                         dst[n_edges - GROUP:n_edges].rearrange("(p e) -> p e", e=GROUP)).then_inc(dst_in, 16)
            for u in range(RINGS):
                load_index(0, u)
            for u in range(2):
                load_attr(0, u)

            def move_q(c):
                w0, n = c * CW, chunk_windows(c)
                sp.wait_ge(q_lo, c + 1)
                up = min(w0 + n, ODD)
                if up > w0:
                    sp.dma_start(Qp[0:HALF, WIN + w0:WIN + up, :, :], Qp[HALF:P, w0:up, :, :]).then_inc(q_odd, 16)
                lo = max(w0, 1)
                sp.dma_start(Qp[HALF:P, WIN + lo - 1:WIN + w0 + n - 1, :, :], Qp[0:HALF, lo:w0 + n, :, :])\
                    .then_inc(q_odd, 16)

            for c in range(CH):
                if c + RINGS < CH:
                    load_x(c + RINGS)
                n = chunk_windows(c)
                sp.wait_ge(kv_out, min(2 * (c + 1), -(-WIN // 2)))
                if c < CH - 1:
                    sp.dma_start(kv_table[c * CW * P:(c * CW + n) * P, :].rearrange("(w p) d -> p w d", p=P),
                                 kv[:, c % RINGS, 0:n, :]).then_inc(kv_stored[c % RINGS], 16)
                else:
                    sp.dma_start(kv_table[(WIN - 1) * P:n_nodes, :], kv[0:LAST_NODES, c % RINGS, 0, :])\
                        .then_inc(kv_stored[c % RINGS], 16)
            sp.wait_ge(unturned, 3)
            for c in range(CH):
                move_q(c)
            sp.wait_ge(x_pad, 1)
            sp.dma_start(x_res[:, 0:WIN - 1, :], x[0:(WIN - 1) * P, :].rearrange("(w p) d -> p w d", p=P))\
                .then_inc(x_res_in, 16)
            sp.dma_start(x_res[0:LAST_NODES, WIN - 1, :], x[(WIN - 1) * P:n_nodes, :]).then_inc(x_res_in, 16)
            for u in (2, 3):
                load_attr(0, u)

            def load_group(b, u):
                load_index(b, u)
                load_attr(b, u)

            with sp.Fori(1, B_LAST) as b:
                for u in range(RINGS):
                    load_group(b, u)
            for g in range(B_LAST * RINGS, G):
                load_group(g // RINGS, g % RINGS)

            sp.wait_ge(table_ok, 1)
            sp.wait_ge(first_ok, 1)
            with sp.If(sp.value_load(table[0:1, 1, G:G + 1], min_val=0, max_val=G) > 0):
                with sp.Fori(0, G) as g:
                    nth = sp.value_load(table[0:1, 1, bass.ds(g, 1)], min_val=0, max_val=G)
                    nth_next = sp.value_load(table[0:1, 1, bass.ds(g + 1, 1)], min_val=0, max_val=G)
                    with sp.If(nth_next > nth):
                        first = sp.value_load(table[0:1, 2, bass.ds(g, 1)], min_val=0, max_val=n_edges - GROUP)
                        sp.wait_ge(s_added, nth * WIN + 1)
                        sp.sem_inc(stray_go, 1)
                        sp.dma_start(src_idx[:, 0, :], src[bass.ds(first, GROUP)]
                                     .rearrange("(p t) -> p t", p=P).bitcast(U32)).then_inc(s_idx, 16)
                        sp.dma_start(attr[:, 0, :, :], edge_attr[bass.ds(first, GROUP), :]
                                     .rearrange("(p t) d -> p t d", p=P)).then_inc(s_attr, 16)

            sp.wait_ge(all_added, 1)
            for c in range(FC):
                w0, w1 = c * FW, (c + 1) * FW
                up = min(w1, ODD)
                sp.dma_start(moved[HALF:P, w0:up, :], acc[0:HALF, WIN + w0:WIN + up, :]).then_inc(moved_in[c], 16)
                lo = max(w0, 1)
                sp.dma_start(moved[0:HALF, lo:w1, :], acc[HALF:P, WIN + lo - 1:WIN + w1 - 1, :])\
                    .then_inc(moved_in[c], 16)
            for c in range(FC):
                sp.wait_ge(norm_ok, c + 1)
                if c < FC - 1:
                    sp.dma_start(out[c * FW * P:(c + 1) * FW * P, :].rearrange("(w p) d -> p w d", p=P),
                                 acc[:, c * FW:(c + 1) * FW, 0:dim]).then_inc(stored, 16)
                else:
                    sp.dma_start(out[c * FW * P:(WIN - 1) * P, :].rearrange("(w p) d -> p w d", p=P),
                                 acc[:, c * FW:WIN - 1, 0:dim]).then_inc(stored, 16)
                    sp.dma_start(out[(WIN - 1) * P:n_nodes, :], acc[0:LAST_NODES, WIN - 1, 0:dim])\
                        .then_inc(stored, 16)
            sp.wait_ge(stored, 16 * (FC + 1))

        @block.gpsimd
        def _(pool):
            nc.gpsimd.memset(ident[:, :], 0.0).then_inc(id_zero, 1)
            nc.gpsimd.iota(iota[:, :], [[1, P]], base=0, channel_multiplier=0,
                           allow_small_or_imprecise_dtypes=True).then_inc(const_ready, 1)
            nc.gpsimd.iota(table[0:1, 2, 0:G - 1], [[GROUP, G - 1]], base=0, channel_multiplier=0)
            nc.gpsimd.iota(table[0:1, 2, G - 1:G], [[0, 1]], base=edge0(G - 1), channel_multiplier=0)\
                .then_inc(first_ok, 1)
            pool.wait_ge(id_zero, 1)
            nc.gpsimd.affine_select(out=ident[:, :], in_=ident[:, :], compare_op=ALU.not_equal, fill=1.0, base=0,
                                    pattern=[[-1, P]], channel_multiplier=1).then_inc(const_ready, 1)
            pool.wait_ge(prep, 6)
            last = local_rows[:, GC - 1, :]
            nc.gpsimd.affine_select(out=last, in_=last, compare_op=ALU.is_ge, fill=NOT_AN_EDGE,
                                    base=LAST_ROW * 2 * GROUP - REPEATED, pattern=[[1, GROUP]],
                                    channel_multiplier=-2 * GROUP).then_inc(masked, 1)
            nc.gpsimd.memset(acc[:, :, :], 0.0).then_inc(acc_zero, 1)

            def gather(b, u):
                g = b * RINGS + u
                pool.wait_ge(idx_in[u], b * 16 + 16)
                if past(g, RINGS):
                    pool.wait_ge(msg_ok, g - RINGS + 1)
                pool.sem_inc(go, 1)
                for t in range(TILES):
                    nc.gpsimd.indirect_dma_start(
                        out=kv[:, u, t, :], out_offset=None, in_=kv_table,
                        in_offset=bass.IndirectOffsetOnAxis(ap=src_idx[:, u, t:t + 1], axis=0)).then_inc(kv_in[u], 16)

            for i in range(RINGS):
                pool.wait_ge(kv_stored[i], 16 * len(range(i, CH, RINGS)))
            for u in range(RINGS):
                gather(0, u)
            with pool.Fori(1, B_LAST) as b:
                for u in range(RINGS):
                    gather(b, u)
            for g in range(B_LAST * RINGS, G):
                gather(g // RINGS, g % RINGS)

            pool.wait_ge(table_ok, 1)
            with pool.If(pool.value_load(table[0:1, 1, G:G + 1], min_val=0, max_val=G) > 0):
                with pool.Fori(0, G) as g:
                    nth = pool.value_load(table[0:1, 1, bass.ds(g, 1)], min_val=0, max_val=G)
                    nth_next = pool.value_load(table[0:1, 1, bass.ds(g + 1, 1)], min_val=0, max_val=G)
                    with pool.If(nth_next > nth):
                        pool.wait_ge(s_idx, nth * 16 + 16)
                        pool.sem_inc(go, 1)
                        for t in range(TILES):
                            nc.gpsimd.indirect_dma_start(
                                out=kv[:, 0, t, :], out_offset=None, in_=kv_table,
                                in_offset=bass.IndirectOffsetOnAxis(ap=src_idx[:, 0, t:t + 1], axis=0))\
                                .then_inc(s_kv, 16)

            def add_x(c):
                w = slice(c * FW, (c + 1) * FW)
                pool.wait_ge(attn, c + 1)
                nc.gpsimd.tensor_tensor(acc[:, w, 0:dim], acc[:, w, 0:dim], x_res[:, w, :], ALU.add).then_inc(resid, 1)

            pool.wait_ge(all_added, 1)
            pool.wait_ge(x_res_in, 32)
            for c in range(FC):
                pool.wait_ge(moved_in[c], 32)
                w = slice(c * FW, (c + 1) * FW)
                nc.gpsimd.tensor_tensor(acc[:, w, :], acc[:, w, :], moved[:, w, :], ALU.add).then_inc(total, 1)
                if c >= 1:
                    add_x(c - 1)
            add_x(FC - 1)

        @block.tensor
        def _(pe):
            pe.wait_ge(const_ready, 2)
            pe.wait_ge(w_in, 64)

            def turn_local(rnd):
                if rnd == 0:
                    pe.wait_ge(masked, 1)
                else:
                    pe.wait_ge(unturned, rnd)
                for c in range(GC):
                    cols = slice(c * P, (c + 1) * P)
                    if rnd < 2:
                        for i in range(2):
                            edges = local_rows[:, c, :].rearrange("g (p t) -> g t p", t=TILES)[:, 2 * rnd + i, :]
                            last = nc.tensor.transpose(psQ[:, i, cols], edges, ident[:, :])
                    else:
                        nc.tensor.matmul(psQ[0:1, 0, cols], slot_col[:, c:c + 1], ident[:, :], start=True, stop=True)
                        last = nc.tensor.matmul(psQ[:, 1, cols], home_col[:, c:c + 1].to_broadcast([P, P]),
                                                ident[:, :], start=True, stop=True)
                last.then_inc(turned, 1)

            def kv_products(c):
                pe.wait_ge(xT_ok, c + 1)
                for i in range(0, chunk_windows(c), 2):
                    pair = c * (CW // 2) + i // 2
                    if pair >= 2:
                        pe.wait_ge(kv_out, pair - 1)
                    for w in range(c * CW + i, min(c * CW + i + 2, WIN)):
                        o = (w % 2) * 2 * dim
                        last = nc.tensor.matmul(psE[:, pair % 2, o:o + 2 * dim], xT[:, w * P:(w + 1) * P],
                                                w_kv[:, :], start=True, stop=True)
                    last.then_inc(kv_mm, 1)

            def q_products(c):
                if c >= 2:
                    pe.wait_ge(q_sub, c - 1)
                for i in range(chunk_windows(c)):
                    w = c * CW + i
                    last = nc.tensor.matmul(psW[:, c % 2, i * P:(i + 1) * P], xT[:, w * P:(w + 1) * P], w_q[:, :],
                                            start=True, stop=True)
                last.then_inc(q_mm, 1)

            for c in range(CH):
                pe.wait_ge(x_at[c % RINGS], 16 * (c // RINGS + 1))
                if c >= 2:
                    pe.wait_ge(xT_ok, c - 1)
                for i in range(chunk_windows(c)):
                    nodes = x_in[:, c % RINGS, i, :] if c < CH - 1 else x_last
                    last = nc.tensor.transpose(psX[c % 2][:, i * P:(i + 1) * P], nodes, ident[:, :])
                last.then_inc(x_tr, 1)
                if c >= 1:
                    kv_products(c - 1)
                    if c - 1 < EARLY:
                        q_products(c - 1)
                if PREP <= c < PREP + 3:
                    turn_local(c - PREP)
            kv_products(CH - 1)
            for c in range(EARLY, CH):
                q_products(c)

            def turn_attr(b, u):
                g = b * RINGS + u
                pe.wait_ge(attr_in[u % 2], b * 32 + (u // 2) * 16 + 16)
                if past(g, 1):
                    pe.wait_ge(attrT_ok, g)
                for t in range(TILES):
                    last = nc.tensor.transpose(psT[:, t * P:(t + 1) * P], attr[:, u % 2, t, :], ident[:, :])
                last.then_inc(attr_tr, 1)

            def edge_products(b, u):
                g = b * RINGS + u
                pe.wait_ge(attrT_ok, g + 1)
                if past(g, 2):
                    pe.wait_ge(ke, g - 1)
                for t in range(TILES):
                    last = nc.tensor.matmul(psE[:, u % 2, t * P:(t + 1) * P], attrT[:, u % 2, t * P:(t + 1) * P],
                                            w_e[:, :], start=True, stop=True)
                last.then_inc(e_mm, 1)

            def turn_hot(b, u):
                g = b * RINGS + u
                pe.wait_ge(hot_ok, g + 1)
                if past(g, 1):
                    pe.wait_ge(hotT_ok, g)
                for t in range(TILES):
                    last = nc.tensor.transpose(psH[:, t * P:(t + 1) * P], hot[:, u, t, :], ident[:, :])
                last.then_inc(hot_tr, 1)

            def select_q(b, u):
                g = b * RINGS + u
                slot = pe.value_load(table[0:1, 0, bass.ds(g, 1)], min_val=0, max_val=SLOTS - 1)
                pe.wait_ge(hotT_ok, g + 1)
                if past(g, 2):
                    pe.wait_ge(keq, g - 1)
                for t in range(TILES):
                    for part in range(3):
                        last = nc.tensor.matmul(psQ[:, u % 2, t * P:(t + 1) * P], hotT[:, u % 2, t * P:(t + 1) * P],
                                                Qp[:, bass.ds(slot, 1), part, :].rearrange("p a d -> p (a d)"),
                                                start=(part == 0), stop=(part == 2))
                last.then_inc(q_sel, 1)

            def sum_messages(b, u):
                g = b * RINGS + u
                pe.wait_ge(msg_ok, g + 1)
                if past(g, 2):
                    pe.wait_ge(added, g - 1)
                for t in range(TILES):
                    last = nc.tensor.matmul(psW[:, u % 2, 0:MW], hot[:, u, t, :], msg[:, u % 2, t, :],
                                            start=(t == 0), stop=(t == TILES - 1))
                last.then_inc(sums, 1)

            def step(b, u):
                b1, u1 = b + (u + 1) // RINGS, (u + 1) % RINGS
                b2, u2 = b + (u + 2) // RINGS, (u + 2) % RINGS
                peeled = isinstance(b, int)
                if not peeled or b2 * RINGS + u2 < G:
                    turn_attr(b2, u2)
                    turn_hot(b2, u2)
                if not peeled or b1 * RINGS + u1 < G:
                    edge_products(b1, u1)
                    select_q(b1, u1)
                sum_messages(b, u)

            pe.wait_ge(slots_ok, 1)
            pe.wait_ge(q_lo, CH)
            pe.wait_ge(q_odd, 16 * q_odd_dmas)
            for u in range(2):
                turn_attr(0, u)
                turn_hot(0, u)
            edge_products(0, 0)
            select_q(0, 0)
            pe.wait_ge(stray_ok, 1)
            nc.tensor.matmul(psW[0:1, 1, 0:G], ones_col[:, :], stray[:, :], start=True, stop=True).then_inc(stray_mm, 1)
            step(0, 0)
            pe.wait_ge(count, 1)
            for u in range(1, RINGS):
                step(0, u)
            with pe.Fori(1, B_LAST) as b:
                for u in range(RINGS):
                    step(b, u)
            for g in range(B_LAST * RINGS, G):
                step(g // RINGS, g % RINGS)

            pe.wait_ge(table_ok, 1)
            with pe.If(pe.value_load(table[0:1, 1, G:G + 1], min_val=0, max_val=G) > 0):
                with pe.Fori(0, G) as g:
                    nth = pe.value_load(table[0:1, 1, bass.ds(g, 1)], min_val=0, max_val=G)
                    nth_next = pe.value_load(table[0:1, 1, bass.ds(g + 1, 1)], min_val=0, max_val=G)
                    with pe.If(nth_next > nth):
                        pe.wait_ge(s_attr, nth * 16 + 16)
                        for t in range(TILES):
                            last = nc.tensor.transpose(psT[:, t * P:(t + 1) * P], attr[:, 0, t, :], ident[:, :])
                        last.then_inc(s_tr, 1)
                        pe.wait_ge(s_attrT, nth + 1)
                        for t in range(TILES):
                            last = nc.tensor.matmul(psE[:, 0, t * P:(t + 1) * P], attrT[:, 0, t * P:(t + 1) * P],
                                                    w_e[:, :], start=True, stop=True)
                        last.then_inc(s_e, 1)
                        with pe.Fori(0, WIN) as w:
                            k = nth * WIN + w + 1
                            pe.wait_ge(s_hot, k)
                            for t in range(TILES):
                                last = nc.tensor.transpose(psH[:, t * P:(t + 1) * P], hot[:, 0, t, :], ident[:, :])
                            last.then_inc(s_hot_tr, 1)
                            pe.wait_ge(s_hotT, k)
                            for t in range(TILES):
                                for part in range(3):
                                    last = nc.tensor.matmul(
                                        psQ[:, 0, t * P:(t + 1) * P], hotT[:, 0, t * P:(t + 1) * P],
                                        Qp[:, bass.ds(w, 1), part, :].rearrange("p a d -> p (a d)"),
                                        start=(part == 0), stop=(part == 2))
                            last.then_inc(s_q, 1)
                            pe.wait_ge(s_msg, k)
                            for t in range(TILES):
                                last = nc.tensor.matmul(psW[:, 0, 0:MW], hot[:, 0, t, :], msg[:, 0, t, :],
                                                        start=(t == 0), stop=(t == TILES - 1))
                            last.then_inc(s_sums, 1)

        @block.scalar
        def _(act):
            weights = ((w_kv[:, 0:dim], wk), (w_kv[:, dim:2 * dim], wv), (w_q[:, :], wq), (w_e[:, :], we))
            for to, weight in weights:
                act.dma_start(to, weight).then_inc(w_in, 16)

            def copy_x(c):
                n = chunk_windows(c) * P
                act.wait_ge(x_tr, c + 1)
                nc.scalar.activation(xT[:, c * CW * P:c * CW * P + n], psX[c % 2][:, 0:n], ACT.Copy).then_inc(xT_ok, 1)

            def copy_turned(rnd):
                act.wait_ge(turned, rnd + 1)
                if rnd < 2:
                    for i in range(2):
                        last = nc.scalar.activation(local[:, 2 * rnd + i, :], psQ[:, i, 0:G], ACT.Copy)
                else:
                    last = nc.scalar.activation(home[:, :], psQ[:, 1, :], ACT.Copy)
                last.then_inc(unturned, 1)

            def q_view(c, part):
                return Qp[:, c * CW:c * CW + chunk_windows(c), part, :]

            def first_part(c):
                act.wait_ge(q_mm, c + 1)
                n = chunk_windows(c)
                nc.scalar.activation(q_view(c, 0), psW[:, c % 2, 0:n * P].rearrange("p (w d) -> p w d", d=dim),
                                     ACT.Copy).then_inc(q_hi, 1)

            def second_part(c):
                act.wait_ge(q_sub, c + 1)
                n = chunk_windows(c)
                nc.scalar.activation(q_view(c, 1), q_rest[:, c % 2, 0:n * P].rearrange("p (w d) -> p w d", d=dim),
                                     ACT.Copy).then_inc(q_mid, 1)

            for c in range(CH):
                copy_x(c)
                if 2 <= c < EARLY + 2:
                    first_part(c - 2)
                if 3 <= c < EARLY + 3:
                    second_part(c - 3)
                if PREP <= c < PREP + 3:
                    copy_turned(c - PREP)
            first_part(EARLY)
            for c in range(EARLY, CH):
                if c + 1 < CH:
                    first_part(c + 1)
                second_part(c)
            act.wait_ge(q_lo, CH)

            def mark(b, u):
                g = b * RINGS + u
                if past(g, RINGS):
                    act.wait_ge(sums, g - RINGS + 1)
                for t in range(TILES):
                    last = nc.scalar.activation(hot[:, u, t, :], iota[:, :], ACT.Abs, scale=-1.0,
                                                bias=local[:, t, bass.ds(g, 1)])
                last.then_inc(apart, 1)
                act.wait_ge(apart, g + 1)
                nc.scalar.activation(hot[:, u, :, :], hot[:, u, :, :], ACT.Relu, scale=-1.0 / NOT_AN_EDGE,
                                     bias=one[:, 0:1])\
                    .then_inc(hot_ok, 1)

            def copy_attr(b, u):
                g = b * RINGS + u
                act.wait_ge(attr_tr, g + 1)
                if past(g, 2):
                    act.wait_ge(e_mm, g - 1)
                nc.scalar.activation(attrT[:, u % 2, :], psT[:, :], ACT.Copy).then_inc(attrT_ok, 1)

            def copy_hot(b, u):
                g = b * RINGS + u
                act.wait_ge(hot_tr, g + 1)
                if past(g, 2):
                    act.wait_ge(q_sel, g - 1)
                nc.scalar.activation(hotT[:, u % 2, :], psH[:, :], ACT.Copy).then_inc(hotT_ok, 1)

            def exponentials(b, u):
                g = b * RINGS + u
                act.wait_ge(clip, g + 1)
                if past(g, 2):
                    act.wait_ge(sums, g - 1)
                nc.scalar.activation(msg[:, u % 2, :, dim:MW], clipped[:, :].rearrange("p (t h) -> p t h", h=HEADS),
                                     ACT.Exp, scale=SCALE).then_inc(exp_ok, 1)

            def step(b, u):
                b2, u2 = b + (u + 2) // RINGS, (u + 2) % RINGS
                b3, u3 = b + (u + 3) // RINGS, (u + 3) % RINGS
                peeled = isinstance(b, int)
                if not peeled or b2 * RINGS + u2 < G:
                    copy_attr(b2, u2)
                    copy_hot(b2, u2)
                exponentials(b, u)
                if not peeled or b3 * RINGS + u3 < G:
                    mark(b3, u3)

            act.wait_ge(const_ready, 2)
            act.wait_ge(prep, 7)
            for u in range(3):
                mark(0, u)
            for u in range(2):
                copy_attr(0, u)
                copy_hot(0, u)
            for u in range(RINGS):
                step(0, u)
            with act.Fori(1, B_LAST) as b:
                for u in range(RINGS):
                    step(b, u)
            for g in range(B_LAST * RINGS, G):
                step(g // RINGS, g % RINGS)

            act.wait_ge(table_ok, 1)
            with act.If(act.value_load(table[0:1, 1, G:G + 1], min_val=0, max_val=G) > 0):
                with act.Fori(0, G) as g:
                    nth = act.value_load(table[0:1, 1, bass.ds(g, 1)], min_val=0, max_val=G)
                    nth_next = act.value_load(table[0:1, 1, bass.ds(g + 1, 1)], min_val=0, max_val=G)
                    with act.If(nth_next > nth):
                        act.wait_ge(s_tr, nth + 1)
                        nc.scalar.activation(attrT[:, 0, :], psT[:, :], ACT.Copy).then_inc(s_attrT, 1)
                        with act.Fori(0, WIN) as w:
                            k = nth * WIN + w + 1
                            act.wait_ge(s_hot_tr, k)
                            nc.scalar.activation(hotT[:, 0, :], psH[:, :], ACT.Copy).then_inc(s_hotT, 1)
                            act.wait_ge(s_clip, k)
                            nc.scalar.activation(msg[:, 0, :, dim:MW],
                                                 clipped[:, :].rearrange("p (t h) -> p t h", h=HEADS),
                                                 ACT.Exp, scale=SCALE).then_inc(s_exp, 1)

            for c in range(FC):
                act.wait_ge(aggr, c + 1)
                nc.scalar.activation(std[:, c % 2, :], mean_var[:, c % 2, :, 1], ACT.Sqrt, bias=ln_eps[:, 0:1])\
                    .then_inc(std_ok, 1)
                act.wait_ge(shift_ok, c + 1)
                for i in range(FW):
                    w = c * FW + i
                    last = nc.scalar.activation(acc[:, w, 0:dim], acc[:, w, 0:dim], ACT.Identity,
                                                bias=shift[:, c % 2, i:i + 1], scale=rstd[:, c % 2, i:i + 1])
                last.then_inc(norm_ok, 1)

        @block.vector
        def _(dve):
            nc.vector.memset(dst_rows[:, GC - 1, :], 0).then_inc(rows_zero, 1)
            nc.vector.memset(x_last[LAST_NODES // 32 * 32:P, :], 0.0).then_inc(x_zero, 1)
            nc.vector.memset(ln_eps[:, :], LN_EPS)
            nc.vector.memset(one[:, :], 1.0)
            nc.vector.memset(ones_col[:, :], 1.0)
            dve.wait_ge(dst_in, 48)
            nc.vector.tensor_scalar(hcol[:, :], dst_rows[:, :, 0], 6, None, ALU.logical_shift_right).then_inc(prep, 1)
            dve.wait_ge(prep, 1)
            nc.vector.tensor_scalar(hcol[:, :], hcol[:, :], 2 * (WIN - 1), None, ALU.min).then_inc(prep, 1)
            dve.wait_ge(prep, 2)
            nc.vector.tensor_scalar(home_col[:, :], hcol[:, :], float(HALF), None, ALU.mult).then_inc(prep, 1)
            nc.vector.tensor_scalar(odd_col[:, :], hcol[:, :], 1, None, ALU.bitwise_and)
            nc.vector.tensor_scalar(pair_col[:, :], hcol[:, :], 1, None, ALU.logical_shift_right).then_inc(prep, 1)
            dve.wait_ge(prep, 4)
            nc.vector.scalar_tensor_tensor(slot_col[:, :], odd_col[:, :], float(WIN), pair_col[:, :],
                                           ALU.mult, ALU.add).then_inc(prep, 1)
            for c in range(GC):
                last = nc.vector.tensor_scalar(local_rows[:, c, :], dst_rows[:, c, :], home_col[:, c:c + 1], None,
                                               ALU.subtract)
            last.then_inc(prep, 2)

            def copy_kv(pair):
                c, o = pair // (CW // 2), pair % (CW // 2) * 2
                n = min(2, WIN - 2 * pair)
                dve.wait_ge(kv_mm, pair + 1)
                if c >= RINGS and o == 0:
                    dve.wait_ge(kv_stored[c % RINGS], c // RINGS * 16)
                nc.vector.tensor_copy(kv[:, c % RINGS, o:o + n, :],
                                      psE[:, pair % 2, 0:n * 2 * dim].rearrange("p (w d) -> p w d", w=n))\
                    .then_inc(kv_out, 1)

            def q_view(c, part):
                return Qp[:, c * CW:c * CW + chunk_windows(c), part, :]

            def rest_view(c):
                return q_rest[:, c % 2, 0:chunk_windows(c) * P].rearrange("p (w d) -> p w d", d=dim)

            def after_first(c):
                dve.wait_ge(q_hi, c + 1)
                if c >= 2:
                    dve.wait_ge(q_lo, c - 1)
                full = psW[:, c % 2, 0:chunk_windows(c) * P].rearrange("p (w d) -> p w d", d=dim)
                nc.vector.tensor_tensor(rest_view(c), full, q_view(c, 0), ALU.subtract).then_inc(q_sub, 1)

            def third_part(c):
                dve.wait_ge(q_mid, c + 1)
                nc.vector.tensor_tensor(q_view(c, 2), rest_view(c), q_view(c, 1), ALU.subtract).then_inc(q_lo, 1)

            for c in range(1, CH + 1):
                for pair in range((c - 1) * (CW // 2), min(c * (CW // 2), -(-WIN // 2))):
                    copy_kv(pair)
                if 2 <= c < EARLY + 2:
                    after_first(c - 2)
                if 3 <= c < EARLY + 3:
                    third_part(c - 3)
                if c == PREP + 3:
                    dve.wait_ge(turned, 3)
                    nc.vector.tensor_copy(table[0:1, 0, 0:G], psQ[0:1, 0, 0:G]).then_inc(slots_ok, 1)
            after_first(EARLY)
            for c in range(EARLY, CH):
                if c + 1 < CH:
                    after_first(c + 1)
                third_part(c)
            dve.wait_ge(q_mm, CH)
            nc.vector.memset(x_res[LAST_NODES // 32 * 32:P, WIN - 1, :], 0.0).then_inc(x_pad, 1)
            dve.wait_ge(unturned, 2)
            by_group = local[:, :, :].rearrange("p t g -> p g t")
            nc.vector.tensor_reduce(least, by_group, AX.X, ALU.min).then_inc(range_ok, 1)
            nc.vector.tensor_reduce(most, by_group, AX.X, ALU.max).then_inc(range_ok, 1)
            dve.wait_ge(range_ok, 2)
            nc.vector.tensor_scalar(least, least, 0.0, None, ALU.is_lt).then_inc(range_ok, 1)
            dve.wait_ge(range_ok, 3)
            nc.vector.scalar_tensor_tensor(stray[:, :], most, float(P - 1), least, ALU.is_gt, ALU.max)\
                .then_inc(stray_ok, 1)

            def count_strays():
                dve.wait_ge(stray_mm, 1)
                nc.vector.tensor_scalar(stray_row, psW[0:1, 1, 0:G], 0.0, None, ALU.is_gt).then_inc(count, 1)
                dve.wait_ge(count, 1)
                nc.vector.tensor_tensor_scan(stray_row, stray_row, stray_row, 0.0, ALU.add, ALU.bypass)\
                    .then_inc(count, 1)
                nc.vector.memset(table[0:1, 1, 0:1], 0)
                dve.wait_ge(count, 2)
                nc.vector.tensor_copy(table[0:1, 1, 1:G + 1], stray_row).then_inc(table_ok, 1)
                dve.wait_ge(table_ok, 1)

            def scores(b, u):
                g = b * RINGS + u
                dve.wait_ge(e_mm, g + 1)
                dve.wait_ge(kv_in[u], b * TILES * 16 + TILES * 16)
                tiles = prod[:, :].rearrange("p (t d) -> p t d", d=dim)
                nc.vector.tensor_tensor(tiles, kv[:, u, :, 0:dim],
                                        psE[:, u % 2, :].rearrange("p (t d) -> p t d", d=dim), ALU.mult).then_inc(ke, 1)
                dve.wait_ge(ke, g + 1)
                dve.wait_ge(q_sel, g + 1)
                nc.vector.tensor_tensor(prod[:, :], prod[:, :], psQ[:, u % 2, :], ALU.mult).then_inc(keq, 1)
                dve.wait_ge(keq, g + 1)
                if past(g, 1):
                    dve.wait_ge(clip, g)
                nc.vector.tensor_reduce(score[:, :], prod[:, :].rearrange("p (a d) -> p a d", d=DH), AX.X, ALU.add)\
                    .then_inc(dot, 1)
                dve.wait_ge(dot, g + 1)
                if past(g, 1):
                    dve.wait_ge(exp_ok, g)
                nc.vector.tensor_scalar(clipped[:, :], score[:, :], SCORE_LIMIT / SCALE, -SCORE_LIMIT / SCALE,
                                        ALU.min, ALU.max).then_inc(clip, 1)

            def messages(b, u):
                g = b * RINGS + u
                dve.wait_ge(exp_ok, g + 1)
                nc.vector.tensor_tensor(per_head(msg[:, u % 2, :, 0:dim]), per_head(kv[:, u, :, dim:2 * dim]),
                                        msg[:, u % 2, :, dim:MW].unsqueeze(3).to_broadcast([P, TILES, HEADS, DH]),
                                        ALU.mult).then_inc(msg_ok, 1)

            def add_sums(b, u):
                g = b * RINGS + u
                slot = dve.value_load(table[0:1, 0, bass.ds(g, 1)], min_val=0, max_val=SLOTS - 1)
                dve.wait_ge(sums, g + 1)
                if past(g, 1):
                    dve.wait_ge(added, g)
                where = acc[:, bass.ds(slot, 1), :].rearrange("p a m -> p (a m)")
                nc.vector.tensor_tensor(where, psW[:, u % 2, 0:MW], where, ALU.add).then_inc(added, 1)

            def step(b, u):
                b0, u0 = b + (u - 1) // RINGS, (u - 1) % RINGS
                scores(b, u)
                messages(b, u)
                if not isinstance(b, int) or b0 >= 0:
                    add_sums(b0, u0)

            dve.wait_ge(acc_zero, 1)
            step(0, 0)
            count_strays()
            for u in range(1, RINGS):
                step(0, u)
            with dve.Fori(1, B_LAST) as b:
                for u in range(RINGS):
                    step(b, u)
            for g in range(B_LAST * RINGS, G):
                step(g // RINGS, g % RINGS)
            add_sums((G - 1) // RINGS, (G - 1) % RINGS)
            dve.wait_ge(added, G)
            nc.vector.memset(cur[:, :, :], BIG).then_inc(s_added, 1)

            dve.wait_ge(table_ok, 1)
            with dve.If(dve.value_load(table[0:1, 1, G:G + 1], min_val=0, max_val=G) > 0):
                with dve.Fori(0, G) as g:
                    nth = dve.value_load(table[0:1, 1, bass.ds(g, 1)], min_val=0, max_val=G)
                    nth_next = dve.value_load(table[0:1, 1, bass.ds(g + 1, 1)], min_val=0, max_val=G)
                    with dve.If(nth_next > nth):
                        dve.wait_ge(s_added, nth * WIN + 1)
                        where = local[:, :, bass.ds(g, 1)].rearrange("p t a -> p (t a)")
                        c0 = nth * 4 + 1
                        nc.vector.tensor_scalar(cur[:, 0, :], where, 0.0, None, ALU.is_ge)
                        nc.vector.tensor_scalar(cur[:, 1, :], where, float(P - 1), BIG, ALU.is_le, ALU.mult)\
                            .then_inc(s_cur, 1)
                        dve.wait_ge(s_cur, c0)
                        nc.vector.tensor_tensor(cur[:, 1, :], cur[:, 1, :], cur[:, 0, :], ALU.mult).then_inc(s_cur, 1)
                        dve.wait_ge(s_cur, c0 + 1)
                        nc.vector.tensor_tensor(cur[:, 0, :], cur[:, 1, :], where, ALU.add).then_inc(s_cur, 1)
                        dve.wait_ge(s_cur, c0 + 2)
                        nc.vector.tensor_scalar(cur[:, 0, :], cur[:, 0, :], home[:, bass.ds(g, 1)], None, ALU.add)\
                            .then_inc(s_cur, 1)
                        dve.wait_ge(s_e, nth + 1)
                        dve.wait_ge(s_kv, nth * (TILES * 16) + TILES * 16)
                        nc.vector.tensor_tensor(prod[:, :].rearrange("p (t d) -> p t d", d=dim), kv[:, 0, :, 0:dim],
                                                psE[:, 0, :].rearrange("p (t d) -> p t d", d=dim), ALU.mult)\
                            .then_inc(s_ke, 1)
                        keq_w = hot[:, 1, :, :].rearrange("p t d -> p (t d)")
                        with dve.Fori(0, WIN) as w:
                            k = nth * WIN + w + 1
                            dve.wait_ge(s_cur, c0 + 3)
                            for t in range(TILES):
                                last = nc.vector.tensor_scalar(hot[:, 0, t, :], iota[:, :], cur[:, 0, t:t + 1], None,
                                                               ALU.is_equal)
                            last.then_inc(s_hot, 1)
                            dve.wait_ge(s_ke, nth + 1)
                            dve.wait_ge(s_q, k)
                            nc.vector.tensor_tensor(keq_w, prod[:, :], psQ[:, 0, :], ALU.mult).then_inc(s_keq, 1)
                            dve.wait_ge(s_keq, k)
                            nc.vector.tensor_reduce(score[:, :], keq_w.rearrange("p (a d) -> p a d", d=DH), AX.X,
                                                    ALU.add).then_inc(s_dot, 1)
                            dve.wait_ge(s_dot, k)
                            nc.vector.tensor_scalar(clipped[:, :], score[:, :], SCORE_LIMIT / SCALE,
                                                    -SCORE_LIMIT / SCALE, ALU.min, ALU.max).then_inc(s_clip, 1)
                            dve.wait_ge(s_exp, k)
                            nc.vector.tensor_tensor(
                                per_head(msg[:, 0, :, 0:dim]), per_head(kv[:, 0, :, dim:2 * dim]),
                                msg[:, 0, :, dim:MW].unsqueeze(3).to_broadcast([P, TILES, HEADS, DH]), ALU.mult)\
                                .then_inc(s_msg, 1)
                            dve.wait_ge(s_sums, k)
                            at = acc[:, bass.ds(w, 1), :].rearrange("p a m -> p (a m)")
                            nc.vector.tensor_scalar(cur[:, 0, :], cur[:, 0, :], float(P), None, ALU.subtract)
                            nc.vector.tensor_tensor(at, psW[:, 0, 0:MW], at, ALU.add).then_inc(s_added, 1)
                            dve.wait_ge(s_added, k + 1)

            nc.vector.memset(moved[0:HALF, 0, :], 0.0)
            nc.vector.memset(moved[HALF:P, WIN - 1, :], 0.0).then_inc(moved_zero, 1)
            dve.wait_ge(moved_zero, 1)
            nc.vector.memset(score[:, :], 0.0).then_inc(all_added, 1)

            def scale_and_shift(c):
                dve.wait_ge(std_ok, c + 1)
                if c >= 2:
                    dve.wait_ge(norm_ok, c - 1)
                nc.vector.reciprocal(rstd[:, c % 2, :], std[:, c % 2, :]).then_inc(rstd_ok, 1)
                dve.wait_ge(rstd_ok, c + 1)
                nc.vector.scalar_tensor_tensor(shift[:, c % 2, :], mean_var[:, c % 2, :, 0], -1.0, rstd[:, c % 2, :],
                                               ALU.mult, ALU.mult).then_inc(shift_ok, 1)

            def attention(c):
                w = slice(c * FW, (c + 1) * FW)
                dve.wait_ge(total, c + 1)
                if c >= 1:
                    dve.wait_ge(attn, c)
                nc.vector.tensor_scalar(zinv[:, :, :], acc[:, w, dim:MW], Z_EPS, None, ALU.add).then_inc(zadd, 1)
                dve.wait_ge(zadd, c + 1)
                nc.vector.reciprocal(zinv[:, :, :], zinv[:, :, :]).then_inc(zrec, 1)
                dve.wait_ge(zrec, c + 1)
                nc.vector.tensor_tensor(per_head(acc[:, w, 0:dim]), per_head(acc[:, w, 0:dim]),
                                        zinv[:, :, :].unsqueeze(3).to_broadcast([P, FW, HEADS, DH]), ALU.mult)\
                    .then_inc(attn, 1)

            def statistics(c):
                dve.wait_ge(resid, c + 1)
                if c >= 1:
                    dve.wait_ge(aggr, c)
                for i in range(FW):
                    last = nc.vector.bn_stats(stats[:, i, :], acc[:, c * FW + i, 0:dim])
                last.then_inc(stat, 1)
                dve.wait_ge(stat, c + 1)
                if c >= 2:
                    dve.wait_ge(std_ok, c - 1)
                    dve.wait_ge(shift_ok, c - 1)
                for i in range(FW):
                    last = nc.vector.bn_aggr(mean_var[:, c % 2, i, :], stats[:, i, :])
                last.then_inc(aggr, 1)

            for c in range(FC + 2):
                if c < FC:
                    attention(c)
                if c >= 2:
                    scale_and_shift(c - 2)
                if 1 <= c <= FC:
                    statistics(c - 1)


_INS = ["x", "src", "dst", "edge_attr_128", "L0_gnn_WQ", "L0_gnn_WK", "L0_gnn_WV", "L0_gnn_WE"]
_OUT = ((6250, 128), "float32")


def kernel(**inputs):
    import numpy as _np
    import concourse.bacc as _bacc
    from concourse import mybir as _mybir
    from concourse.bass_utils import run_bass_kernel_spmd as _run

    nc = _bacc.Bacc("TRN2", target_bir_lowering=False, num_devices=1)
    arrays, args = {}, []
    for name in _INS:
        a = _np.ascontiguousarray(inputs[name])
        arrays[f"in_{name}_dram"] = a
        args.append(nc.dram_tensor(f"in_{name}_dram", a.shape, _mybir.dt.from_np(a.dtype), kind="ExternalInput").ap())
    args.append(nc.dram_tensor("out_0_dram", _OUT[0], _mybir.dt.from_np(_np.dtype(_OUT[1])), kind="ExternalOutput").ap())
    graph_attention_layernorm(nc, *args)
    r = _run(nc, [arrays], core_ids=[0])
    return r.results[0]["out_0_dram"]
```

```python
from contextlib import ExitStack

import concourse.bass as bass
from concourse import mybir

P = 128
F32 = mybir.dt.float32
BF16 = mybir.dt.bfloat16
I32 = mybir.dt.int32
U32 = mybir.dt.uint32
ALU = mybir.AluOpType
ACT = mybir.ActivationFunctionType
AX = mybir.AxisListType

HEADS = 8
RINGS = 8
HOTS = 4
ATTRS = 4
LAG = 4
BIG = 1.0e6
HALF_WINDOW, SLOT, ODD_BIT, STRAYS, FIRST, OPEN = range(6)
COLUMN = (1, 3, 1)
NOT_AN_EDGE = 0.5
SCORE_LIMIT = 5.0
Z_EPS = 1e-6
LN_EPS = 1e-5
ROOT_GUESS = 0x5f3759df
NEWTON_STEPS = 3


def past(g, n):
    return g >= n if isinstance(g, int) else True


def graph_attention_layernorm(nc, x, src, dst, edge_attr, wq, wk, wv, we, out):
    n_nodes, dim = x.shape
    n_edges = src.shape[0]
    TILES = 4
    GROUP = TILES * P
    G = -(-n_edges // GROUP)
    REPEATED = G * GROUP - n_edges
    GC = -(-G // P)
    LAST_ROW = (G - 1) % P
    WIN = -(-n_nodes // P)
    ODD = WIN - 1
    SLOTS = WIN + ODD
    LAST_NODES = n_nodes - (WIN - 1) * P
    DH = dim // HEADS
    MW = dim + HEADS
    SCALE = float(DH) ** -0.5
    assert dim == P and SCALE == 0.25
    CW = 4
    CH = -(-WIN // CW)
    HALF = P // 2
    B_LAST = G // RINGS
    EARLY = B_LAST - LAG
    LATE = WIN - EARLY
    RES_WIN = -(-(WIN - 1) // RINGS)
    STAGES = 10 + 3 * NEWTON_STEPS
    assert STAGES <= 3 * RINGS and 0 < LATE <= TILES

    def chunk_windows(c):
        return min(CW, WIN - c * CW)

    q_odd_dmas = sum((c * CW < ODD) + 1 for c in range(CH))

    def edge0(g):
        return min(g * GROUP, n_edges - GROUP) if isinstance(g, int) else g * GROUP

    kv_table = nc.dram_tensor("kv_table", [n_nodes, 2 * dim], F32).ap()

    with ExitStack() as ctx:
        def sb(name, shape, dt=F32):
            return ctx.enter_context(nc.sbuf_tensor(name, shape, dt))

        def pb(name, shape):
            return ctx.enter_context(nc.psum_tensor(name, shape, F32))

        def sem(name):
            return ctx.enter_context(nc.semaphore(name))

        table = sb("table", [1, 6, -(-(G + max(COLUMN)) // 4) * 4], I32)
        xT = sb("xT", [P, WIN * P])
        acc = sb("acc", [P, WIN, MW])
        Qp = sb("Qp", [P, SLOTS, 3, dim], BF16)
        kv = sb("kv", [P, RINGS, TILES, 2 * dim])
        src_idx = sb("src_idx", [P, RINGS, TILES], U32)
        attr = sb("attr", [P, ATTRS, TILES, dim])
        attrT = sb("attrT", [P, 2, GROUP])
        hot = sb("hot", [P, HOTS, TILES, P])
        hotT = sb("hotT", [P, 2, GROUP], BF16)
        prod = sb("prod", [P, GROUP])
        msg = sb("msg", [P, 2, TILES, MW])
        score = sb("score", [P, TILES * HEADS])
        clipped = sb("clipped", [P, TILES * HEADS])
        local = sb("local", [P, TILES, G])
        home = sb("home", [P, GC * P])
        iota = sb("iota", [P, 2, P])
        ident = sb("ident", [P, P])
        w_kv = sb("w_kv", [P, 2 * dim])
        w_q = sb("w_q", [P, dim])
        w_e = sb("w_e", [P, dim])
        pair_col = sb("pair_col", [P, GC], I32)
        int_cols = sb("int_cols", [P, GC, 3], I32)
        place_cols = sb("place_cols", [P, GC, 3])
        home_col = sb("home_col", [P, GC])
        stray = sb("stray", [P, G], BF16)
        ones_col = sb("ones_col", [P, 1], BF16)
        one = sb("one", [P, 1])
        cur = sb("cur", [P, 2, TILES])
        zinv = sb("zinv", [P, LATE, HEADS])
        window_y = sb("window_y", [P, 1, dim])
        stats = sb("stats", [P, LATE, 6])
        mean_var = sb("mean_var", [P, LATE, 2])
        var_eps = sb("var_eps", [P, LATE])
        newton = sb("newton", [P, LATE])
        rstd = sb("rstd", [P, LATE])
        late = sb("late", [1, 1])
        x_in = hot[:, :, :, :]
        x_last = prod[:, 0:dim]
        q_rest = attrT[:, :, :]
        least = msg[:, 0, :, :].rearrange("p t m -> p (t m)")[:, 0:G]
        most = msg[:, 1, :, :].rearrange("p t m -> p (t m)")[:, 0:G]
        place_rows = hotT[0:3, :, :].rearrange("r s e -> r (s e)").bitcast(I32)[:, 0:G]
        stray_row = most[0:1, :]
        late_y = prod[:, 0:LATE * dim].rearrange("p (w d) -> p w d", d=dim)
        redo_cell = table[0:1, HALF_WINDOW, 0:1]
        x_res = xT[:, :].rearrange("p (w d) -> p w d", d=dim)
        rows = Qp[:, :, :, :].rearrange("p s t d -> p (s t d)").bitcast(F32)[:, SLOTS * 3 * dim // 2 - GC * GROUP:]
        dst_rows = rows.bitcast(I32).rearrange("p (c e) -> p c e", c=GC)
        local_rows = rows.rearrange("p (c e) -> p c e", c=GC)
        psT = pb("psT", [P, GROUP])
        psH = pb("psH", [P, GROUP])
        psE = pb("psE", [P, 2, GROUP])
        psQ = pb("psQ", [P, 2, GROUP])
        psW = pb("psW", [P, 2, GROUP])
        psX = [psT, psH]
        turn_bank = [psQ[:, 0, :], psQ[:, 1, :], psT[:, :], psH[:, :]]

        rows_zero = sem("rows_zero")
        x_zero = sem("x_zero")
        id_zero = sem("id_zero")
        const_ready = sem("const_ready")
        first_ok = sem("first_ok")
        acc_zero = sem("acc_zero")
        dst_in = sem("dst_in")
        w_in = sem("w_in")
        x_at = [sem(f"x_at{i}") for i in range(HOTS)]
        prep = sem("prep")
        masked = sem("masked")
        turned = sem("turned")
        unturned = sem("unturned")
        places_ok = sem("places_ok")
        places_in = sem("places_in")
        x_tr = sem("x_tr")
        xT_ok = sem("xT_ok")
        kv_mm = sem("kv_mm")
        kv_out = sem("kv_out")
        kv_stored = [sem(f"kv_stored{i}") for i in range(RINGS)]
        q_mm = sem("q_mm")
        q_hi = sem("q_hi")
        q_sub = sem("q_sub")
        q_mid = sem("q_mid")
        q_lo = sem("q_lo")
        q_odd = sem("q_odd")
        x_pad = sem("x_pad")
        x_res_in = sem("x_res_in")
        range_ok = sem("range_ok")
        stray_ok = sem("stray_ok")
        stray_mm = sem("stray_mm")
        count = sem("count")
        table_ok = sem("table_ok")
        idx_in = [sem(f"idx_in{i}") for i in range(RINGS)]
        attr_in = [sem(f"attr_in{i}") for i in range(ATTRS)]
        kv_in = [sem(f"kv_in{i}") for i in range(RINGS)]
        go = sem("go")
        attr_tr = sem("attr_tr")
        attrT_ok = sem("attrT_ok")
        e_mm = sem("e_mm")
        apart = sem("apart")
        hot_ok = sem("hot_ok")
        hot_tr = sem("hot_tr")
        hotT_ok = sem("hotT_ok")
        q_sel = sem("q_sel")
        ke = sem("ke")
        keq = sem("keq")
        dot = sem("dot")
        clip = sem("clip")
        exp_ok = sem("exp_ok")
        msg_ok = sem("msg_ok")
        sums = sem("sums")
        added = sem("added")
        stray_go = sem("stray_go")
        s_idx = sem("s_idx")
        s_attr = sem("s_attr")
        s_kv = sem("s_kv")
        s_tr = sem("s_tr")
        s_attrT = sem("s_attrT")
        s_e = sem("s_e")
        s_ke = sem("s_ke")
        s_cur = sem("s_cur")
        s_hot = sem("s_hot")
        s_hot_tr = sem("s_hot_tr")
        s_hotT = sem("s_hotT")
        s_q = sem("s_q")
        s_keq = sem("s_keq")
        s_dot = sem("s_dot")
        s_clip = sem("s_clip")
        s_exp = sem("s_exp")
        s_msg = sem("s_msg")
        s_sums = sem("s_sums")
        s_added = sem("s_added")
        finish_go = sem("finish_go")
        finished = sem("finished")
        refinished = sem("refinished")
        x_again = sem("x_again")
        restored = sem("restored")
        stored = sem("stored")

        def load_row(engine, row, g, n, largest):
            _, values = nc.values_load_multi_w_load_instructions(
                table[0:1, row, bass.ds(g + COLUMN[row], n)], engines=(engine,), min_val=0, max_val=largest)
            return values

        def per_head(ap):
            return ap.rearrange("p t (h d) -> p t h d", h=HEADS)

        block = ctx.enter_context(nc.Block())

        @block.sync
        def _(sp):
            def load_x(c):
                n = chunk_windows(c)
                if c < CH - 1:
                    if c >= HOTS:
                        sp.wait_ge(x_tr, c - HOTS + 1)
                    sp.dma_start(x_in[:, c % HOTS, 0:n, :], x[c * CW * P:(c * CW + n) * P, :]
                                 .rearrange("(w p) d -> p w d", p=P)).then_inc(x_at[c % HOTS], 16)
                else:
                    sp.wait_ge(x_zero, 1)
                    sp.dma_start(x_last[0:LAST_NODES, :], x[(WIN - 1) * P:n_nodes, :]).then_inc(x_at[c % HOTS], 16)

            def load_index(b, u):
                g = b * RINGS + u
                if past(g, RINGS):
                    sp.wait_ge(kv_in[u], b * TILES * 16)
                sp.dma_start(src_idx[:, u, :], src[bass.ds(edge0(g), GROUP)].rearrange("(p t) -> p t", p=P)
                             .bitcast(U32)).then_inc(idx_in[u], 16)

            def load_attr(b, u):
                g = b * RINGS + u
                if past(g, ATTRS):
                    sp.wait_ge(attr_tr, g - ATTRS + 1)
                sp.dma_start(attr[:, u % ATTRS, :, :], edge_attr[bass.ds(edge0(g), GROUP), :]
                             .rearrange("(p t) d -> p t d", p=P)).then_inc(attr_in[u % ATTRS], 16)

            for c in range(HOTS):
                load_x(c)
            full = (GC - 1) * P
            sp.dma_start(dst_rows[:, 0:GC - 1, :],
                         dst[0:full * GROUP].rearrange("(c p e) -> p c e", p=P, e=GROUP)).then_inc(dst_in, 16)
            sp.wait_ge(rows_zero, 1)
            sp.dma_start(dst_rows[0:LAST_ROW, GC - 1, :],
                         dst[full * GROUP:(G - 1) * GROUP].rearrange("(p e) -> p e", e=GROUP)).then_inc(dst_in, 16)
            sp.dma_start(dst_rows[LAST_ROW:LAST_ROW + 1, GC - 1, :],
                         dst[n_edges - GROUP:n_edges].rearrange("(p e) -> p e", e=GROUP)).then_inc(dst_in, 16)
            for u in range(RINGS):
                load_index(0, u)
            for u in range(ATTRS):
                load_attr(0, u)

            def move_q(c):
                w0, n = c * CW, chunk_windows(c)
                sp.wait_ge(q_lo, c + 1)
                up = min(w0 + n, ODD)
                if up > w0:
                    sp.dma_start(Qp[HALF:P, WIN + w0:WIN + up, :, :], Qp[HALF:P, w0:up, :, :]).then_inc(q_odd, 16)
                lo = max(w0, 1)
                sp.dma_start(Qp[0:HALF, WIN + lo - 1:WIN + w0 + n - 1, :, :], Qp[0:HALF, lo:w0 + n, :, :])\
                    .then_inc(q_odd, 16)

            for c in range(CH):
                if c + HOTS < CH:
                    load_x(c + HOTS)
                n = chunk_windows(c)
                sp.wait_ge(kv_out, min(2 * (c + 1), -(-WIN // 2)))
                if c < CH - 1:
                    sp.dma_start(kv_table[c * CW * P:(c * CW + n) * P, :].rearrange("(w p) d -> p w d", p=P),
                                 kv[:, c % RINGS, 0:n, :]).then_inc(kv_stored[c % RINGS], 16)
                else:
                    sp.dma_start(kv_table[(WIN - 1) * P:n_nodes, :], kv[0:LAST_NODES, c % RINGS, 0, :])\
                        .then_inc(kv_stored[c % RINGS], 16)
            sp.wait_ge(places_ok, 1)
            for row in range(3):
                sp.dma_start(table[0:1, row, COLUMN[row]:COLUMN[row] + G], place_rows[row:row + 1, :])\
                    .then_inc(places_in, 16)
            sp.wait_ge(unturned, 1)
            for c in range(CH):
                move_q(c)
            sp.wait_ge(x_pad, 1)
            sp.dma_start(x_res[0:LAST_NODES, WIN - 1, :], x[(WIN - 1) * P:n_nodes, :]).then_inc(x_res_in, 16)

            def load_group(b, u):
                load_index(b, u)
                load_attr(b + (u - ATTRS) // RINGS, (u - ATTRS) % RINGS)

            def load_turn(b):
                for u in range(RINGS):
                    load_group(b, u)

            def window_rows(w):
                return x_res[:, bass.ds(w, 1), :].rearrange("p a d -> p (a d)")

            def store_window(w):
                sp.wait_ge(finished, w * STAGES + STAGES)
                sp.dma_start(out[bass.ds(w * P, P), :], window_rows(w)).then_inc(stored, 16)

            for u in range(RINGS):
                load_group(1, u)
                first, behind = u * RES_WIN, min((u + 1) * RES_WIN, WIN - 1)
                sp.dma_start(x_res[:, first:behind, :], x[first * P:behind * P, :].rearrange("(w p) d -> p w d", p=P))\
                    .then_inc(x_res_in, 16)
            with sp.Fori(2, LAG + 2) as b:
                load_turn(b)
            with sp.Fori(LAG + 2, B_LAST) as b:
                load_turn(b)
                store_window(b - (LAG + 2))
            for g in range(B_LAST * RINGS, G):
                load_group(g // RINGS, g % RINGS)
            for g in range(G - ATTRS, G):
                load_attr(g // RINGS, g % RINGS)
            for w in range(EARLY - 2, EARLY):
                store_window(w)

            sp.wait_ge(table_ok, 1)
            sp.wait_ge(first_ok, 2)
            with sp.If(sp.value_load(table[0:1, STRAYS, G:G + 1], min_val=0, max_val=G) > 0):
                with sp.Fori(0, G) as g:
                    nth = sp.value_load(table[0:1, STRAYS, bass.ds(g, 1)], min_val=0, max_val=G)
                    nth_next = sp.value_load(table[0:1, STRAYS, bass.ds(g + 1, 1)], min_val=0, max_val=G)
                    with sp.If(nth_next > nth):
                        first = sp.value_load(table[0:1, FIRST, bass.ds(g, 1)], min_val=0, max_val=n_edges - GROUP)
                        sp.wait_ge(s_added, nth * WIN + 1)
                        sp.sem_inc(stray_go, 1)
                        sp.dma_start(src_idx[:, 0, :], src[bass.ds(first, GROUP)]
                                     .rearrange("(p t) -> p t", p=P).bitcast(U32)).then_inc(s_idx, 16)
                        sp.dma_start(attr[:, 0, :, :], edge_attr[bass.ds(first, GROUP), :]
                                     .rearrange("(p t) d -> p t d", p=P)).then_inc(s_attr, 16)

            sp.wait_ge(finished, (EARLY + 1) * STAGES)
            sp.dma_start(out[EARLY * P:(WIN - 1) * P, :].rearrange("(w p) d -> p w d", p=P),
                         x_res[:, EARLY:WIN - 1, :]).then_inc(stored, 16)
            sp.dma_start(out[(WIN - 1) * P:n_nodes, :], x_res[0:LAST_NODES, WIN - 1, :]).then_inc(stored, 16)
            sp.wait_ge(stored, 16 * (EARLY + 2))

            with sp.If(sp.value_load(redo_cell, min_val=0, max_val=G) > 0):
                with sp.Fori(0, EARLY) as w:
                    sp.dma_start(window_rows(w), x[bass.ds(w * P, P), :]).then_inc(x_again, 16)
                    sp.wait_ge(refinished, w * STAGES + STAGES)
                    sp.sem_inc(stray_go, 1)
                    sp.dma_start(out[bass.ds(w * P, P), :], window_rows(w)).then_inc(restored, 16)
                sp.wait_ge(restored, 16 * EARLY)

        @block.gpsimd
        def _(pool):
            nc.gpsimd.memset(ident[:, :], 0.0).then_inc(id_zero, 1)
            pool.wait_ge(id_zero, 1)
            nc.gpsimd.affine_select(out=ident[:, :], in_=ident[:, :], compare_op=ALU.not_equal, fill=1.0, base=0,
                                    pattern=[[-1, P]], channel_multiplier=1).then_inc(const_ready, 1)

            def count_up(out, base, n):
                return nc.gpsimd.iota(out, [[1, n]], base=base, channel_multiplier=0,
                                      allow_small_or_imprecise_dtypes=True)

            count_up(iota[:, 0, :], 0, P)
            count_up(iota[:, 1, 0:HALF], HALF, HALF)
            count_up(iota[:, 1, HALF:P], 0, HALF).then_inc(const_ready, 1)
            nc.gpsimd.iota(table[0:1, FIRST, 0:G - 1], [[GROUP, G - 1]], base=0, channel_multiplier=0)
            nc.gpsimd.iota(table[0:1, FIRST, G - 1:G], [[0, 1]], base=edge0(G - 1), channel_multiplier=0)\
                .then_inc(first_ok, 1)
            nc.gpsimd.iota(table[0:1, OPEN, 0:B_LAST * RINGS].rearrange("a (b u) -> a b u", u=RINGS),
                           [[2, B_LAST], [0, RINGS]], base=2 * (1 - LAG), channel_multiplier=0)
            nc.gpsimd.iota(table[0:1, OPEN, B_LAST * RINGS:G + 1], [[0, G + 1 - B_LAST * RINGS]], base=2 * EARLY,
                           channel_multiplier=0).then_inc(first_ok, 1)
            pool.wait_ge(prep, 4)
            last = local_rows[:, GC - 1, :]
            nc.gpsimd.affine_select(out=last, in_=last, compare_op=ALU.is_ge, fill=NOT_AN_EDGE,
                                    base=LAST_ROW * 2 * GROUP - REPEATED, pattern=[[1, GROUP]],
                                    channel_multiplier=-2 * GROUP).then_inc(masked, 1)
            nc.gpsimd.memset(acc[:, :, :], 0.0).then_inc(acc_zero, 1)

            def gather(b, u):
                g = b * RINGS + u
                pool.wait_ge(idx_in[u], b * 16 + 16)
                if past(g, RINGS):
                    pool.wait_ge(msg_ok, g - RINGS + 1)
                pool.sem_inc(go, 1)
                for t in range(TILES):
                    nc.gpsimd.indirect_dma_start(
                        out=kv[:, u, t, :], out_offset=None, in_=kv_table,
                        in_offset=bass.IndirectOffsetOnAxis(ap=src_idx[:, u, t:t + 1], axis=0)).then_inc(kv_in[u], 16)

            for i in range(RINGS):
                pool.wait_ge(kv_stored[i], 16 * len(range(i, CH, RINGS)))
            for u in range(RINGS):
                gather(0, u)
            with pool.Fori(1, B_LAST) as b:
                for u in range(RINGS):
                    gather(b, u)
            for g in range(B_LAST * RINGS, G):
                gather(g // RINGS, g % RINGS)

            pool.wait_ge(table_ok, 1)
            with pool.If(pool.value_load(table[0:1, STRAYS, G:G + 1], min_val=0, max_val=G) > 0):
                with pool.Fori(0, G) as g:
                    nth = pool.value_load(table[0:1, STRAYS, bass.ds(g, 1)], min_val=0, max_val=G)
                    nth_next = pool.value_load(table[0:1, STRAYS, bass.ds(g + 1, 1)], min_val=0, max_val=G)
                    with pool.If(nth_next > nth):
                        pool.wait_ge(s_idx, nth * 16 + 16)
                        pool.sem_inc(go, 1)
                        for t in range(TILES):
                            nc.gpsimd.indirect_dma_start(
                                out=kv[:, 0, t, :], out_offset=None, in_=kv_table,
                                in_offset=bass.IndirectOffsetOnAxis(ap=src_idx[:, 0, t:t + 1], axis=0))\
                                .then_inc(s_kv, 16)

        @block.tensor
        def _(pe):
            pe.wait_ge(const_ready, 1)

            def turn_local():
                pe.wait_ge(masked, 1)
                pe.wait_ge(xT_ok, CH)
                for t in range(TILES):
                    for c in range(GC):
                        edges = local_rows[:, c, :].rearrange("g (p t) -> g t p", t=TILES)[:, t, :]
                        last = nc.tensor.transpose(turn_bank[t][:, c * P:(c + 1) * P], edges, ident[:, :])
                last.then_inc(turned, 1)

            def turn_columns():
                pe.wait_ge(prep, 7)
                for c in range(GC):
                    cols = slice(c * P, (c + 1) * P)
                    nc.tensor.matmul(psW[0:3, 0, cols], place_cols[:, c, :], ident[:, :], start=True, stop=True)
                    last = nc.tensor.matmul(psW[:, 1, cols], home_col[:, c:c + 1].to_broadcast([P, P]),
                                            ident[:, :], start=True, stop=True)
                last.then_inc(turned, 1)

            def kv_products(c):
                pe.wait_ge(xT_ok, c + 1)
                if c == 0:
                    pe.wait_ge(w_in, 64)
                for i in range(0, chunk_windows(c), 2):
                    pair = c * (CW // 2) + i // 2
                    if pair >= 2:
                        pe.wait_ge(kv_out, pair - 1)
                    for w in range(c * CW + i, min(c * CW + i + 2, WIN)):
                        o = (w % 2) * 2 * dim
                        last = nc.tensor.matmul(psE[:, pair % 2, o:o + 2 * dim], xT[:, w * P:(w + 1) * P],
                                                w_kv[:, :], start=True, stop=True)
                    last.then_inc(kv_mm, 1)

            def q_products(c):
                if c >= 2:
                    pe.wait_ge(q_sub, c - 1)
                for i in range(chunk_windows(c)):
                    w = c * CW + i
                    last = nc.tensor.matmul(psW[:, c % 2, i * P:(i + 1) * P], xT[:, w * P:(w + 1) * P], w_q[:, :],
                                            start=True, stop=True)
                last.then_inc(q_mm, 1)

            for c in range(CH):
                pe.wait_ge(x_at[c % HOTS], 16 * (c // HOTS + 1))
                if c >= 2:
                    pe.wait_ge(xT_ok, c - 1)
                for i in range(chunk_windows(c)):
                    nodes = x_in[:, c % HOTS, i, :] if c < CH - 1 else x_last
                    last = nc.tensor.transpose(psX[c % 2][:, i * P:(i + 1) * P], nodes, ident[:, :])
                last.then_inc(x_tr, 1)
                if c >= 1:
                    kv_products(c - 1)
            kv_products(CH - 1)
            turn_local()
            turn_columns()
            pe.wait_ge(places_ok, 1)
            pe.wait_ge(unturned, 2)
            for c in range(CH):
                q_products(c)

            def turn_attr(b, u):
                g = b * RINGS + u
                pe.wait_ge(attr_in[u % ATTRS], (b * (RINGS // ATTRS) + u // ATTRS) * 16 + 16)
                if past(g, 1):
                    pe.wait_ge(attrT_ok, g)
                for t in range(TILES):
                    last = nc.tensor.transpose(psT[:, t * P:(t + 1) * P], attr[:, u % ATTRS, t, :], ident[:, :])
                last.then_inc(attr_tr, 1)

            def edge_products(b, u):
                g = b * RINGS + u
                pe.wait_ge(attrT_ok, g + 1)
                if past(g, 2):
                    pe.wait_ge(ke, g - 1)
                for t in range(TILES):
                    last = nc.tensor.matmul(psE[:, u % 2, t * P:(t + 1) * P], attrT[:, u % 2, t * P:(t + 1) * P],
                                            w_e[:, :], start=True, stop=True)
                last.then_inc(e_mm, 1)

            def turn_hot(b, u):
                g = b * RINGS + u
                pe.wait_ge(hot_ok, g + 1)
                if past(g, 1):
                    pe.wait_ge(hotT_ok, g)
                for t in range(TILES):
                    last = nc.tensor.transpose(psH[:, t * P:(t + 1) * P], hot[:, u % HOTS, t, :], ident[:, :])
                last.then_inc(hot_tr, 1)

            def load_slots(g, n):
                return load_row(mybir.EngineType.PE, SLOT, g, n, SLOTS - 1)

            def select_q(b, u, slot):
                g = b * RINGS + u
                pe.wait_ge(hotT_ok, g + 1)
                if past(g, 2):
                    pe.wait_ge(keq, g - 1)
                for t in range(TILES):
                    for part in range(3):
                        last = nc.tensor.matmul(psQ[:, u % 2, t * P:(t + 1) * P], hotT[:, u % 2, t * P:(t + 1) * P],
                                                Qp[:, bass.ds(slot, 1), part, :].rearrange("p a d -> p (a d)"),
                                                start=(part == 0), stop=(part == 2))
                last.then_inc(q_sel, 1)

            def sum_messages(b, u):
                g = b * RINGS + u
                pe.wait_ge(msg_ok, g + 1)
                if past(g, 2):
                    pe.wait_ge(added, g - 1)
                for t in range(TILES):
                    last = nc.tensor.matmul(psW[:, u % 2, 0:MW], hot[:, u % HOTS, t, :], msg[:, u % 2, t, :],
                                            start=(t == 0), stop=(t == TILES - 1))
                last.then_inc(sums, 1)

            def step(b, u, next_slot):
                b1, u1 = b + (u + 1) // RINGS, (u + 1) % RINGS
                b2, u2 = b + (u + 2) // RINGS, (u + 2) % RINGS
                peeled = isinstance(b, int)
                if not peeled or b2 * RINGS + u2 < G:
                    turn_attr(b2, u2)
                    turn_hot(b2, u2)
                if not peeled or b1 * RINGS + u1 < G:
                    edge_products(b1, u1)
                    select_q(b1, u1, next_slot)
                sum_messages(b, u)

            turn_attr(0, 0)
            turn_hot(0, 0)
            turn_attr(0, 1)
            edge_products(0, 0)
            pe.wait_ge(stray_ok, 1)
            nc.tensor.matmul(psW[0:1, 1, 0:G], ones_col[:, :], stray[:, :], start=True, stop=True).then_inc(stray_mm, 1)
            turn_hot(0, 1)
            pe.wait_ge(places_in, 48)
            slots = load_slots(0, 1) + load_slots(1, RINGS)
            pe.wait_ge(q_lo, CH)
            pe.wait_ge(q_odd, 16 * q_odd_dmas)
            select_q(0, 0, slots[0])
            step(0, 0, slots[1])
            pe.wait_ge(count, 1)
            for u in range(1, RINGS):
                step(0, u, slots[u + 1])
            with pe.Fori(1, B_LAST) as b:
                slots = load_slots(b * RINGS + 1, RINGS)
                for u in range(RINGS):
                    step(b, u, slots[u])
            slots = load_slots(B_LAST * RINGS + 1, G - B_LAST * RINGS - 1)
            for g in range(B_LAST * RINGS, G):
                step(g // RINGS, g % RINGS, slots[g - B_LAST * RINGS] if g + 1 < G else None)

            pe.wait_ge(table_ok, 1)
            with pe.If(pe.value_load(table[0:1, STRAYS, G:G + 1], min_val=0, max_val=G) > 0):
                with pe.Fori(0, G) as g:
                    nth = pe.value_load(table[0:1, STRAYS, bass.ds(g, 1)], min_val=0, max_val=G)
                    nth_next = pe.value_load(table[0:1, STRAYS, bass.ds(g + 1, 1)], min_val=0, max_val=G)
                    with pe.If(nth_next > nth):
                        pe.wait_ge(s_attr, nth * 16 + 16)
                        for t in range(TILES):
                            last = nc.tensor.transpose(psT[:, t * P:(t + 1) * P], attr[:, 0, t, :], ident[:, :])
                        last.then_inc(s_tr, 1)
                        pe.wait_ge(s_attrT, nth + 1)
                        for t in range(TILES):
                            last = nc.tensor.matmul(psE[:, 0, t * P:(t + 1) * P], attrT[:, 0, t * P:(t + 1) * P],
                                                    w_e[:, :], start=True, stop=True)
                        last.then_inc(s_e, 1)
                        with pe.Fori(0, WIN) as w:
                            k = nth * WIN + w + 1
                            pe.wait_ge(s_hot, k)
                            for t in range(TILES):
                                last = nc.tensor.transpose(psH[:, t * P:(t + 1) * P], hot[:, 0, t, :], ident[:, :])
                            last.then_inc(s_hot_tr, 1)
                            pe.wait_ge(s_hotT, k)
                            for t in range(TILES):
                                for part in range(3):
                                    last = nc.tensor.matmul(
                                        psQ[:, 0, t * P:(t + 1) * P], hotT[:, 0, t * P:(t + 1) * P],
                                        Qp[:, bass.ds(w, 1), part, :].rearrange("p a d -> p (a d)"),
                                        start=(part == 0), stop=(part == 2))
                            last.then_inc(s_q, 1)
                            pe.wait_ge(s_msg, k)
                            for t in range(TILES):
                                last = nc.tensor.matmul(psW[:, 0, 0:MW], hot[:, 0, t, :], msg[:, 0, t, :],
                                                        start=(t == 0), stop=(t == TILES - 1))
                            last.then_inc(s_sums, 1)

        @block.scalar
        def _(act):
            weights = ((w_kv[:, 0:dim], wk), (w_kv[:, dim:2 * dim], wv), (w_q[:, :], wq), (w_e[:, :], we))
            for to, weight in weights:
                act.dma_start(to, weight).then_inc(w_in, 16)

            def copy_x(c):
                n = chunk_windows(c) * P
                act.wait_ge(x_tr, c + 1)
                nc.scalar.activation(xT[:, c * CW * P:c * CW * P + n], psX[c % 2][:, 0:n], ACT.Copy).then_inc(xT_ok, 1)

            def copy_turned():
                act.wait_ge(turned, 1)
                for t in range(TILES):
                    last = nc.scalar.activation(local[:, t, :], turn_bank[t][:, 0:G], ACT.Copy)
                last.then_inc(unturned, 1)
                act.wait_ge(turned, 2)
                nc.scalar.activation(home[:, :], psW[:, 1, :], ACT.Copy).then_inc(unturned, 1)

            def q_view(c, part):
                return Qp[:, c * CW:c * CW + chunk_windows(c), part, :]

            def first_part(c):
                act.wait_ge(q_mm, c + 1)
                n = chunk_windows(c)
                nc.scalar.activation(q_view(c, 0), psW[:, c % 2, 0:n * P].rearrange("p (w d) -> p w d", d=dim),
                                     ACT.Copy).then_inc(q_hi, 1)

            def second_part(c):
                act.wait_ge(q_sub, c + 1)
                n = chunk_windows(c)
                nc.scalar.activation(q_view(c, 1), q_rest[:, c % 2, 0:n * P].rearrange("p (w d) -> p w d", d=dim),
                                     ACT.Copy).then_inc(q_mid, 1)

            for c in range(CH):
                copy_x(c)
            copy_turned()
            first_part(0)
            for c in range(CH):
                if c + 1 < CH:
                    first_part(c + 1)
                second_part(c)

            def load_odd(g, n):
                return load_row(mybir.EngineType.Activation, ODD_BIT, g, n, 1)

            def mark(b, u, odd):
                g = b * RINGS + u
                if past(g, HOTS):
                    act.wait_ge(sums, g - HOTS + 1)
                nodes = iota[:, bass.ds(odd, 1), :].rearrange("p a n -> p (a n)")
                for t in range(TILES):
                    last = nc.scalar.activation(hot[:, u % HOTS, t, :], nodes, ACT.Abs, scale=-1.0,
                                                bias=local[:, t, bass.ds(g, 1)])
                last.then_inc(apart, 1)
                act.wait_ge(apart, g + 1)
                slot = hot[:, u % HOTS, :, :]
                nc.scalar.activation(slot, slot, ACT.Relu, scale=-1.0 / NOT_AN_EDGE, bias=one[:, 0:1])\
                    .then_inc(hot_ok, 1)

            def copy_attr(b, u):
                g = b * RINGS + u
                act.wait_ge(attr_tr, g + 1)
                if past(g, 2):
                    act.wait_ge(e_mm, g - 1)
                nc.scalar.activation(attrT[:, u % 2, :], psT[:, :], ACT.Copy).then_inc(attrT_ok, 1)

            def copy_hot(b, u):
                g = b * RINGS + u
                act.wait_ge(hot_tr, g + 1)
                if past(g, 2):
                    act.wait_ge(q_sel, g - 1)
                nc.scalar.activation(hotT[:, u % 2, :], psH[:, :], ACT.Copy).then_inc(hotT_ok, 1)

            def exponentials(b, u):
                g = b * RINGS + u
                act.wait_ge(clip, g + 1)
                if past(g, 2):
                    act.wait_ge(sums, g - 1)
                nc.scalar.activation(msg[:, u % 2, :, dim:MW], clipped[:, :].rearrange("p (t h) -> p t h", h=HEADS),
                                     ACT.Exp, scale=SCALE).then_inc(exp_ok, 1)

            def step(b, u, odd):
                b2, u2 = b + (u + 2) // RINGS, (u + 2) % RINGS
                b3, u3 = b + (u + 3) // RINGS, (u + 3) % RINGS
                peeled = isinstance(b, int)
                if not peeled or b2 * RINGS + u2 < G:
                    copy_attr(b2, u2)
                    copy_hot(b2, u2)
                exponentials(b, u)
                if not peeled or b3 * RINGS + u3 < G:
                    mark(b3, u3, odd)

            act.wait_ge(const_ready, 2)
            act.wait_ge(places_in, 48)
            act.wait_ge(prep, 5)
            odd = load_odd(0, 3)
            mark(0, 0, odd[0])
            act.wait_ge(q_lo, CH)
            for u in range(2):
                copy_attr(0, u)
                copy_hot(0, u)
                mark(0, u + 1, odd[u + 1])
            odd = load_odd(3, RINGS)
            for u in range(RINGS):
                step(0, u, odd[u])
            assert (B_LAST - 1) * RINGS + 3 + RINGS <= G
            with act.Fori(1, B_LAST) as b:
                odd = load_odd(b * RINGS + 3, RINGS)
                for u in range(RINGS):
                    step(b, u, odd[u])
            ahead = B_LAST * RINGS + 3
            odd = load_odd(ahead, G - ahead) if ahead < G else ()
            for g in range(B_LAST * RINGS, G):
                step(g // RINGS, g % RINGS, odd[g + 3 - ahead] if g + 3 < G else None)

            act.wait_ge(table_ok, 1)
            with act.If(act.value_load(table[0:1, STRAYS, G:G + 1], min_val=0, max_val=G) > 0):
                with act.Fori(0, G) as g:
                    nth = act.value_load(table[0:1, STRAYS, bass.ds(g, 1)], min_val=0, max_val=G)
                    nth_next = act.value_load(table[0:1, STRAYS, bass.ds(g + 1, 1)], min_val=0, max_val=G)
                    with act.If(nth_next > nth):
                        act.wait_ge(s_tr, nth + 1)
                        nc.scalar.activation(attrT[:, 0, :], psT[:, :], ACT.Copy).then_inc(s_attrT, 1)
                        with act.Fori(0, WIN) as w:
                            k = nth * WIN + w + 1
                            act.wait_ge(s_hot_tr, k)
                            nc.scalar.activation(hotT[:, 0, :], psH[:, :], ACT.Copy).then_inc(s_hotT, 1)
                            act.wait_ge(s_clip, k)
                            nc.scalar.activation(msg[:, 0, :, dim:MW],
                                                 clipped[:, :].rearrange("p (t h) -> p t h", h=HEADS),
                                                 ACT.Exp, scale=SCALE).then_inc(s_exp, 1)

        @block.vector
        def _(dve):
            nc.vector.memset(dst_rows[:, GC - 1, :], 0).then_inc(rows_zero, 1)
            nc.vector.memset(x_last[LAST_NODES // 32 * 32:P, :], 0.0).then_inc(x_zero, 1)
            nc.vector.memset(one[:, :], 1.0)
            nc.vector.memset(ones_col[:, :], 1.0)
            dve.wait_ge(dst_in, 48)
            half_windows = int_cols[:, :, HALF_WINDOW]
            nc.vector.tensor_scalar(half_windows, dst_rows[:, :, 0], 6, None, ALU.logical_shift_right).then_inc(prep, 1)
            dve.wait_ge(prep, 1)
            nc.vector.tensor_scalar(half_windows, half_windows, 2 * (WIN - 1), None, ALU.min).then_inc(prep, 1)
            dve.wait_ge(prep, 2)
            nc.vector.tensor_scalar(home_col[:, :], half_windows, float(HALF), None, ALU.mult).then_inc(prep, 1)
            dve.wait_ge(prep, 3)
            for c in range(GC):
                last = nc.vector.tensor_scalar(local_rows[:, c, :], dst_rows[:, c, :], home_col[:, c:c + 1], None,
                                               ALU.subtract)
            last.then_inc(prep, 1)
            nc.vector.tensor_scalar(pair_col[:, :], half_windows, 1, None, ALU.logical_shift_right)
            nc.vector.tensor_scalar(int_cols[:, :, ODD_BIT], half_windows, 1, None, ALU.bitwise_and).then_inc(prep, 1)
            dve.wait_ge(prep, 5)
            nc.vector.scalar_tensor_tensor(int_cols[:, :, SLOT], int_cols[:, :, ODD_BIT], float(WIN),
                                           pair_col[:, :], ALU.mult, ALU.add).then_inc(prep, 1)
            dve.wait_ge(prep, 6)
            nc.vector.tensor_copy(place_cols[:, :, :], int_cols[:, :, :]).then_inc(prep, 1)

            def copy_kv(pair):
                c, o = pair // (CW // 2), pair % (CW // 2) * 2
                n = min(2, WIN - 2 * pair)
                dve.wait_ge(kv_mm, pair + 1)
                if c >= RINGS and o == 0:
                    dve.wait_ge(kv_stored[c % RINGS], c // RINGS * 16)
                nc.vector.tensor_copy(kv[:, c % RINGS, o:o + n, :],
                                      psE[:, pair % 2, 0:n * 2 * dim].rearrange("p (w d) -> p w d", w=n))\
                    .then_inc(kv_out, 1)

            def q_view(c, part):
                return Qp[:, c * CW:c * CW + chunk_windows(c), part, :]

            def rest_view(c):
                return q_rest[:, c % 2, 0:chunk_windows(c) * P].rearrange("p (w d) -> p w d", d=dim)

            def after_first(c):
                dve.wait_ge(q_hi, c + 1)
                if c >= 2:
                    dve.wait_ge(q_lo, c - 1)
                full = psW[:, c % 2, 0:chunk_windows(c) * P].rearrange("p (w d) -> p w d", d=dim)
                nc.vector.tensor_tensor(rest_view(c), full, q_view(c, 0), ALU.subtract).then_inc(q_sub, 1)

            def third_part(c):
                dve.wait_ge(q_mid, c + 1)
                nc.vector.tensor_tensor(q_view(c, 2), rest_view(c), q_view(c, 1), ALU.subtract).then_inc(q_lo, 1)

            for pair in range(-(-WIN // 2)):
                copy_kv(pair)
            dve.wait_ge(turned, 2)
            nc.vector.tensor_copy(place_rows[:, :], psW[0:3, 0, 0:G]).then_inc(places_ok, 1)
            after_first(0)
            for c in range(CH):
                if c + 1 < CH:
                    after_first(c + 1)
                third_part(c)
            dve.wait_ge(q_mm, CH)
            nc.vector.memset(x_res[LAST_NODES // 32 * 32:P, WIN - 1, :], 0.0).then_inc(x_pad, 1)
            dve.wait_ge(unturned, 1)
            by_group = local[:, :, :].rearrange("p t g -> p g t")
            nc.vector.tensor_reduce(least, by_group, AX.X, ALU.min).then_inc(range_ok, 1)
            nc.vector.tensor_reduce(most, by_group, AX.X, ALU.max).then_inc(range_ok, 1)
            dve.wait_ge(range_ok, 2)
            nc.vector.tensor_scalar(least, least, 0.0, None, ALU.is_lt).then_inc(range_ok, 1)
            dve.wait_ge(range_ok, 3)
            nc.vector.scalar_tensor_tensor(stray[:, :], most, float(P - 1), least, ALU.is_gt, ALU.max)\
                .then_inc(stray_ok, 1)

            def count_strays():
                dve.wait_ge(stray_mm, 1)
                nc.vector.tensor_scalar(stray_row, psW[0:1, 1, 0:G], 0.0, None, ALU.is_gt).then_inc(count, 1)
                dve.wait_ge(count, 1)
                nc.vector.tensor_tensor_scan(stray_row, stray_row, stray_row, 0.0, ALU.add, ALU.bypass)\
                    .then_inc(count, 1)
                nc.vector.memset(table[0:1, STRAYS, 0:1], 0)
                dve.wait_ge(count, 2)
                nc.vector.tensor_copy(table[0:1, STRAYS, 1:G + 1], stray_row).then_inc(count, 1)
                dve.wait_ge(count, 3)
                dve.wait_ge(first_ok, 2)
                half_windows = table[0:1, HALF_WINDOW, COLUMN[HALF_WINDOW]:COLUMN[HALF_WINDOW] + G]
                nc.vector.scalar_tensor_tensor(stray_row, table[0:1, OPEN, 1:G + 1], float(2 * EARLY), half_windows,
                                               ALU.min, ALU.is_gt).then_inc(count, 1)
                dve.wait_ge(count, 4)
                nc.vector.tensor_reduce(late[:, :], stray_row, AX.X, ALU.max).then_inc(count, 1)
                dve.wait_ge(count, 5)
                nc.vector.tensor_tensor(redo_cell, late[:, :], table[0:1, STRAYS, G:G + 1], ALU.max)\
                    .then_inc(table_ok, 1)
                dve.wait_ge(table_ok, 1)

            def scores(b, u, meanwhile):
                g = b * RINGS + u
                dve.wait_ge(e_mm, g + 1)
                dve.wait_ge(kv_in[u], b * TILES * 16 + TILES * 16)
                tiles = prod[:, :].rearrange("p (t d) -> p t d", d=dim)
                nc.vector.tensor_tensor(tiles, kv[:, u, :, 0:dim],
                                        psE[:, u % 2, :].rearrange("p (t d) -> p t d", d=dim), ALU.mult).then_inc(ke, 1)
                meanwhile(0)
                dve.wait_ge(ke, g + 1)
                dve.wait_ge(q_sel, g + 1)
                nc.vector.tensor_tensor(prod[:, :], prod[:, :], psQ[:, u % 2, :], ALU.mult).then_inc(keq, 1)
                meanwhile(1)
                dve.wait_ge(keq, g + 1)
                if past(g, 1):
                    dve.wait_ge(clip, g)
                nc.vector.tensor_reduce(score[:, :], prod[:, :].rearrange("p (a d) -> p a d", d=DH), AX.X, ALU.add)\
                    .then_inc(dot, 1)
                meanwhile(2)
                dve.wait_ge(dot, g + 1)
                if past(g, 1):
                    dve.wait_ge(exp_ok, g)
                nc.vector.tensor_scalar(clipped[:, :], score[:, :], SCORE_LIMIT / SCALE, -SCORE_LIMIT / SCALE,
                                        ALU.min, ALU.max).then_inc(clip, 1)

            def messages(b, u):
                g = b * RINGS + u
                dve.wait_ge(exp_ok, g + 1)
                nc.vector.tensor_tensor(per_head(msg[:, u % 2, :, 0:dim]), per_head(kv[:, u, :, dim:2 * dim]),
                                        msg[:, u % 2, :, dim:MW].unsqueeze(3).to_broadcast([P, TILES, HEADS, DH]),
                                        ALU.mult).then_inc(msg_ok, 1)

            def load_windows(g, n):
                half_windows = load_row(mybir.EngineType.DVE, HALF_WINDOW, g, n, 2 * (WIN - 1))
                return [((h + 1) // 2, h // 2) for h in half_windows]

            def add_sums(b, u, windows):
                g = b * RINGS + u
                low, up = windows
                dve.wait_ge(sums, g + 1)
                if past(g, 1):
                    dve.wait_ge(added, g)
                for half, w in ((slice(0, HALF), low), (slice(HALF, P), up)):
                    where = acc[half, bass.ds(w, 1), :].rearrange("p a m -> p (a m)")
                    last = nc.vector.tensor_tensor(where, psW[half, u % 2, 0:MW], where, ALU.add)
                last.then_inc(added, 1)

            def finish(stage, w, n, rows, mark, before):
                windows = bass.ds(w, n)
                v, t, r = var_eps[:, 0:n], newton[:, 0:n], rstd[:, 0:n]
                r_bits = r.bitcast(I32)
                if stage > 0:
                    dve.wait_ge(mark, before + stage)
                if stage == 0:
                    last = nc.vector.tensor_scalar(zinv[:, 0:n, :], acc[:, windows, dim:MW], Z_EPS, None, ALU.add)
                elif stage == 1:
                    last = nc.vector.reciprocal(zinv[:, 0:n, :], zinv[:, 0:n, :])
                elif stage == 2:
                    last = nc.vector.tensor_tensor(per_head(rows), per_head(acc[:, windows, 0:dim]),
                                                   zinv[:, 0:n, :].unsqueeze(3).to_broadcast([P, n, HEADS, DH]),
                                                   ALU.mult)
                elif stage == 3:
                    last = nc.vector.tensor_tensor(rows, rows, x_res[:, windows, :], ALU.add)
                elif stage == 4:
                    dve.sem_inc(finish_go, 1)
                    for i in range(n):
                        last = nc.vector.bn_stats(stats[:, i, :], rows[:, i, :])
                elif stage == 5:
                    dve.sem_inc(finish_go, 1)
                    for i in range(n):
                        last = nc.vector.bn_aggr(mean_var[:, i, :], stats[:, i, :])
                elif stage == 6:
                    last = nc.vector.tensor_scalar(v, mean_var[:, 0:n, 1], LN_EPS, None, ALU.add)
                elif stage == 7:
                    last = nc.vector.tensor_scalar(r_bits, v.bitcast(I32), 1, None, ALU.logical_shift_right)
                elif stage == 8:
                    last = nc.vector.tensor_scalar(r_bits, r_bits, -1.0, float(ROOT_GUESS), ALU.mult, ALU.add)
                elif stage < STAGES - 1:
                    if stage % 3 == 0:
                        last = nc.vector.tensor_tensor(t, r, v, ALU.mult)
                    elif stage % 3 == 1:
                        last = nc.vector.scalar_tensor_tensor(t, t, -0.5, r, ALU.mult, ALU.mult)
                    else:
                        last = nc.vector.scalar_tensor_tensor(r, t, 1.5, r, ALU.add, ALU.mult)
                else:
                    for i in range(n):
                        y = x_res[:, bass.ds(w + i, 1), :].rearrange("p a d -> p (a d)")
                        last = nc.vector.tensor_scalar(y, rows[:, i, :], mean_var[:, i, 0:1], rstd[:, i:i + 1],
                                                       ALU.subtract, ALU.mult)
                last.then_inc(mark, 1)

            def step(b, u, windows, w=None):
                def finish_some(i):
                    if w is not None and 3 * u + i < STAGES:
                        finish(3 * u + i, w, 1, window_y[:, :, :], finished, w * STAGES)

                scores(b, u, finish_some)
                if past(b * RINGS + u, 1):
                    add_sums(b + (u - 1) // RINGS, (u - 1) % RINGS, windows)
                messages(b, u)

            dve.wait_ge(acc_zero, 1)
            dve.wait_ge(places_in, 48)
            windows = load_windows(0, RINGS - 1)
            count_strays()
            step(0, 0, None)
            for u in range(1, RINGS):
                step(0, u, windows[u - 1])
            with dve.Fori(1, LAG) as b:
                windows = load_windows(b * RINGS - 1, RINGS)
                for u in range(RINGS):
                    step(b, u, windows[u])
            dve.wait_ge(x_res_in, 16 * (RINGS + 1))
            with dve.Fori(LAG, B_LAST) as b:
                windows = load_windows(b * RINGS - 1, RINGS)
                for u in range(RINGS):
                    step(b, u, windows[u], b - LAG)
            windows = load_windows(B_LAST * RINGS - 1, G - B_LAST * RINGS + 1)
            for g in range(B_LAST * RINGS, G):
                step(g // RINGS, g % RINGS, windows[g - B_LAST * RINGS])
            add_sums((G - 1) // RINGS, (G - 1) % RINGS, windows[-1])
            dve.wait_ge(added, G)
            nc.vector.memset(cur[:, :, :], BIG).then_inc(s_added, 1)

            dve.wait_ge(table_ok, 1)
            with dve.If(dve.value_load(table[0:1, STRAYS, G:G + 1], min_val=0, max_val=G) > 0):
                with dve.Fori(0, G) as g:
                    nth = dve.value_load(table[0:1, STRAYS, bass.ds(g, 1)], min_val=0, max_val=G)
                    nth_next = dve.value_load(table[0:1, STRAYS, bass.ds(g + 1, 1)], min_val=0, max_val=G)
                    with dve.If(nth_next > nth):
                        dve.wait_ge(s_added, nth * WIN + 1)
                        where = local[:, :, bass.ds(g, 1)].rearrange("p t a -> p (t a)")
                        c0 = nth * 4 + 1
                        nc.vector.tensor_scalar(cur[:, 0, :], where, 0.0, None, ALU.is_ge)
                        nc.vector.tensor_scalar(cur[:, 1, :], where, float(P - 1), BIG, ALU.is_le, ALU.mult)\
                            .then_inc(s_cur, 1)
                        dve.wait_ge(s_cur, c0)
                        nc.vector.tensor_tensor(cur[:, 1, :], cur[:, 1, :], cur[:, 0, :], ALU.mult).then_inc(s_cur, 1)
                        dve.wait_ge(s_cur, c0 + 1)
                        nc.vector.tensor_tensor(cur[:, 0, :], cur[:, 1, :], where, ALU.add).then_inc(s_cur, 1)
                        dve.wait_ge(s_cur, c0 + 2)
                        nc.vector.tensor_scalar(cur[:, 0, :], cur[:, 0, :], home[:, bass.ds(g, 1)], None, ALU.add)\
                            .then_inc(s_cur, 1)
                        dve.wait_ge(s_e, nth + 1)
                        dve.wait_ge(s_kv, nth * (TILES * 16) + TILES * 16)
                        nc.vector.tensor_tensor(prod[:, :].rearrange("p (t d) -> p t d", d=dim), kv[:, 0, :, 0:dim],
                                                psE[:, 0, :].rearrange("p (t d) -> p t d", d=dim), ALU.mult)\
                            .then_inc(s_ke, 1)
                        keq_w = hot[:, 1, :, :].rearrange("p t d -> p (t d)")
                        with dve.Fori(0, WIN) as w:
                            k = nth * WIN + w + 1
                            dve.wait_ge(s_cur, c0 + 3)
                            for t in range(TILES):
                                last = nc.vector.tensor_scalar(hot[:, 0, t, :], iota[:, 0, :], cur[:, 0, t:t + 1], None,
                                                               ALU.is_equal)
                            last.then_inc(s_hot, 1)
                            dve.wait_ge(s_ke, nth + 1)
                            dve.wait_ge(s_q, k)
                            nc.vector.tensor_tensor(keq_w, prod[:, :], psQ[:, 0, :], ALU.mult).then_inc(s_keq, 1)
                            dve.wait_ge(s_keq, k)
                            nc.vector.tensor_reduce(score[:, :], keq_w.rearrange("p (a d) -> p a d", d=DH), AX.X,
                                                    ALU.add).then_inc(s_dot, 1)
                            dve.wait_ge(s_dot, k)
                            nc.vector.tensor_scalar(clipped[:, :], score[:, :], SCORE_LIMIT / SCALE,
                                                    -SCORE_LIMIT / SCALE, ALU.min, ALU.max).then_inc(s_clip, 1)
                            dve.wait_ge(s_exp, k)
                            nc.vector.tensor_tensor(
                                per_head(msg[:, 0, :, 0:dim]), per_head(kv[:, 0, :, dim:2 * dim]),
                                msg[:, 0, :, dim:MW].unsqueeze(3).to_broadcast([P, TILES, HEADS, DH]), ALU.mult)\
                                .then_inc(s_msg, 1)
                            dve.wait_ge(s_sums, k)
                            at = acc[:, bass.ds(w, 1), :].rearrange("p a m -> p (a m)")
                            nc.vector.tensor_scalar(cur[:, 0, :], cur[:, 0, :], float(P), None, ALU.subtract)
                            nc.vector.tensor_tensor(at, psW[:, 0, 0:MW], at, ALU.add).then_inc(s_added, 1)
                            dve.wait_ge(s_added, k + 1)

            for stage in range(STAGES):
                finish(stage, EARLY, LATE, late_y, finished, EARLY * STAGES)
            with dve.If(dve.value_load(redo_cell, min_val=0, max_val=G) > 0):
                with dve.Fori(0, EARLY) as w:
                    dve.wait_ge(x_again, w * 16 + 16)
                    for stage in range(STAGES):
                        finish(stage, w, 1, window_y[:, :, :], refinished, w * STAGES)


_INS = ["x", "src", "dst", "edge_attr_128", "L0_gnn_WQ", "L0_gnn_WK", "L0_gnn_WV", "L0_gnn_WE"]
_OUT = ((6250, 128), "float32")


def kernel(**inputs):
    import numpy as _np
    import concourse.bacc as _bacc
    from concourse import mybir as _mybir
    from concourse.bass_utils import run_bass_kernel_spmd as _run

    nc = _bacc.Bacc("TRN2", target_bir_lowering=False, num_devices=1)
    arrays, args = {}, []
    for name in _INS:
        a = _np.ascontiguousarray(inputs[name])
        arrays[f"in_{name}_dram"] = a
        args.append(nc.dram_tensor(f"in_{name}_dram", a.shape, _mybir.dt.from_np(a.dtype), kind="ExternalInput").ap())
    args.append(nc.dram_tensor("out_0_dram", _OUT[0], _mybir.dt.from_np(_np.dtype(_OUT[1])), kind="ExternalOutput").ap())
    graph_attention_layernorm(nc, *args)
    r = _run(nc, [arrays], core_ids=[0])
    return r.results[0]["out_0_dram"]
```
